# Optimizing a Trainium2 kernel written in Bass

```python
import numpy as np
import jax
import jax.numpy as jnp

def _softmax(x, axis=-1):
    return jax.nn.softmax(x, axis=axis)

def _gelu(x):
    return jax.nn.gelu(x, approximate=True)

def _silu(x):
    return jax.nn.silu(x)

def _sigmoid(x):
    return jax.nn.sigmoid(x)

def _layernorm(x, axis=-1, eps=1e-05):
    m = jnp.mean(x, axis=axis, keepdims=True)
    v = jnp.var(x, axis=axis, keepdims=True)
    return (x - m) / jnp.sqrt(v + eps)

def _scatter_add(tgt, idx, src, axis=0):
    return tgt.at[idx].add(src)

def _segment_sum(src, seg, n):
    return jax.ops.segment_sum(src, seg, n)
kernel_name = 'mk_xattn_ffn_d1_seqx_r8_1ece05'

def setup_inputs(seed: int=0):
    np.random.seed(seed)
    _w = jnp.asarray

    def _rec_inputs():
        import jax
        import jax.numpy as jnp
        _rk = jax.random.key(seed)
        x = 7.22e-05 + 1 * jax.random.normal(jax.random.fold_in(_rk, 1), (16, 256, 128), jnp.float32)
        _lenS = 256 - jax.random.randint(jax.random.fold_in(_rk, 7), (16,), 0, max(1, 256 // 4) + 1, jnp.int32)
        _lenS2 = 64 - jax.random.randint(jax.random.fold_in(_rk, 8), (16,), 0, max(1, 64 // 4) + 1, jnp.int32)
        _ctx_768P = jax.random.normal(jax.random.fold_in(_rk, 11), (16, 16, 96), jnp.float32)
        _ctx_768c = jax.random.dirichlet(jax.random.fold_in(_rk, 511), 0.3 * jnp.ones((16,), jnp.float32), (16, 64))
        _ctx_768t = jnp.einsum('bsk,bkd->bsd', _ctx_768c, _ctx_768P)
        _ctx_768t = _ctx_768t * jax.lax.rsqrt(jnp.mean(jnp.square(_ctx_768t)) + 1e-12) * 0.953939
        ctx_768 = -0.000191848 + 0.999787 * (_ctx_768t + 0.3 * jax.random.normal(jax.random.fold_in(_rk, 611), (16, 64, 96), jnp.float32))
        return (x, ctx_768)
    x, ctx_768 = _rec_inputs()

    def _L0_xattn_setup():
        import math
        import jax, jax.numpy as jnp
        import numpy as np
        B, SQ, SKV = (4, 256, 256)
        D_EMBED, D_CROSS, D_ATT, N_HEADS = (128, 96, 128, 16)
        D_HEAD = D_ATT // N_HEADS

        def _split_heads(t):
            b, s, _ = t.shape
            return t.reshape(b, s, N_HEADS, D_HEAD).transpose(0, 2, 1, 3)
        key = jax.random.key(seed)
        ks = jax.random.split(key, 10)
        s_e = 1.0 / math.sqrt(D_EMBED)
        s_c = 1.0 / math.sqrt(D_CROSS)
        s_a = 1.0 / math.sqrt(D_ATT)
        return {'x': jax.random.normal(ks[0], (B, SQ, D_EMBED), jnp.float32), 'y': jax.random.normal(ks[1], (B, SKV, D_CROSS), jnp.float32), 'Wq': jax.random.normal(ks[2], (D_EMBED, D_ATT), jnp.float32) * s_e, 'bq': jax.random.normal(ks[3], (D_ATT,), jnp.float32) * 0.01, 'Wk': jax.random.normal(ks[4], (D_CROSS, D_ATT), jnp.float32) * s_c, 'bk': jax.random.normal(ks[5], (D_ATT,), jnp.float32) * 0.01, 'Wv': jax.random.normal(ks[6], (D_CROSS, D_ATT), jnp.float32) * s_c, 'bv': jax.random.normal(ks[7], (D_ATT,), jnp.float32) * 0.01, 'Wo': jax.random.normal(ks[8], (D_ATT, D_EMBED), jnp.float32) * s_a, 'bo': jax.random.normal(ks[9], (D_EMBED,), jnp.float32) * 0.01}
    _L0_xattn_all = _L0_xattn_setup()
    _L0_xattn_in = {k: v for k, v in _L0_xattn_all.items() if k in ('Wq', 'bq', 'Wk', 'bk', 'Wv', 'bv', 'Wo', 'bo')}
    del _L0_xattn_all

    def _L0_ffn_setup():
        import jax, jax.numpy as jnp
        import numpy as np
        from jax import lax
        HIDDEN = 128
        INTER = 64
        E = 64
        K = 6
        G = 8
        TG = 4
        NSH = 2
        ISH = INTER * NSH

        def _moe_forward(hidden_states, gate_w, gate_bias, eg_w, eu_w, ed_w, sg_w, su_w, sd_w):
            B, S, H = hidden_states.shape
            x = hidden_states.reshape(-1, H)
            T = x.shape[0]
            shared = jax.nn.silu(x @ sg_w.T) * (x @ su_w.T) @ sd_w.T
            logits = x @ gate_w.T
            scores = jax.nn.sigmoid(logits) + gate_bias
            group_scores = scores.reshape(T, G, E // G).max(axis=-1)
            _, sel_groups = lax.top_k(group_scores, TG)
            group_mask = jnp.zeros((T, G), scores.dtype).at[jnp.arange(T)[:, None], sel_groups].set(1.0)
            mask = jnp.repeat(group_mask, E // G, axis=1)
            masked_scores = scores * mask
            topk_w, topk_i = lax.top_k(masked_scores, K)
            topk_w = topk_w / (topk_w.sum(axis=-1, keepdims=True) + 1e-08)
            comb = jnp.zeros((T, E), x.dtype).at[jnp.arange(T)[:, None], topk_i].add(topk_w)
            h = jax.nn.silu(jnp.einsum('th,eih->eti', x, eg_w)) * jnp.einsum('th,eih->eti', x, eu_w)
            routed = jnp.einsum('eti,ehi,te->th', h, ed_w, comb)
            return (shared + routed).reshape(B, S, H)
        key = jax.random.key(seed)
        ks = jax.random.split(key, 9)
        s = 0.02
        return {'hidden_states': jax.random.normal(ks[0], (1, 128, HIDDEN), jnp.float32), 'gate_w': jax.random.normal(ks[1], (E, HIDDEN), jnp.float32) * s, 'gate_bias': jnp.zeros((E,), jnp.float32), 'eg_w': jax.random.normal(ks[2], (E, INTER, HIDDEN), jnp.float32) * s, 'eu_w': jax.random.normal(ks[3], (E, INTER, HIDDEN), jnp.float32) * s, 'ed_w': jax.random.normal(ks[4], (E, HIDDEN, INTER), jnp.float32) * s, 'sg_w': jax.random.normal(ks[5], (ISH, HIDDEN), jnp.float32) * s, 'su_w': jax.random.normal(ks[6], (ISH, HIDDEN), jnp.float32) * s, 'sd_w': jax.random.normal(ks[7], (HIDDEN, ISH), jnp.float32) * s}
    _L0_ffn_all = _L0_ffn_setup()
    _L0_ffn_in = {k: v for k, v in _L0_ffn_all.items() if k in ('gate_w', 'gate_bias', 'eg_w', 'eu_w', 'ed_w', 'sg_w', 'su_w', 'sd_w')}
    del _L0_ffn_all
    return {'x': x, 'ctx_768': ctx_768, 'L0_xattn_Wq': _L0_xattn_in['Wq'], 'L0_xattn_bq': _L0_xattn_in['bq'], 'L0_xattn_Wk': _L0_xattn_in['Wk'], 'L0_xattn_bk': _L0_xattn_in['bk'], 'L0_xattn_Wv': _L0_xattn_in['Wv'], 'L0_xattn_bv': _L0_xattn_in['bv'], 'L0_xattn_Wo': _L0_xattn_in['Wo'], 'L0_xattn_bo': _L0_xattn_in['bo'], 'L0_ffn_gate_w': _L0_ffn_in['gate_w'], 'L0_ffn_gate_bias': _L0_ffn_in['gate_bias'], 'L0_ffn_eg_w': _L0_ffn_in['eg_w'], 'L0_ffn_eu_w': _L0_ffn_in['eu_w'], 'L0_ffn_ed_w': _L0_ffn_in['ed_w'], 'L0_ffn_sg_w': _L0_ffn_in['sg_w'], 'L0_ffn_su_w': _L0_ffn_in['su_w'], 'L0_ffn_sd_w': _L0_ffn_in['sd_w']}

def reference(x, ctx_768, L0_xattn_Wq, L0_xattn_bq, L0_xattn_Wk, L0_xattn_bk, L0_xattn_Wv, L0_xattn_bv, L0_xattn_Wo, L0_xattn_bo, L0_ffn_gate_w, L0_ffn_gate_bias, L0_ffn_eg_w, L0_ffn_eu_w, L0_ffn_ed_w, L0_ffn_sg_w, L0_ffn_su_w, L0_ffn_sd_w):
    import jax
    import jax.numpy as jnp

    def _L0_xattn_ref(x, y, Wq, bq, Wk, bk, Wv, bv, Wo, bo):
        import math
        import jax, jax.numpy as jnp
        import numpy as np
        B, SQ, SKV = (4, 256, 256)
        D_EMBED, D_CROSS, D_ATT, N_HEADS = (128, 96, 128, 16)
        D_HEAD = D_ATT // N_HEADS

        def _split_heads(t):
            b, s, _ = t.shape
            return t.reshape(b, s, N_HEADS, D_HEAD).transpose(0, 2, 1, 3)
        q = _split_heads(x @ Wq + bq)
        k = _split_heads(y @ Wk + bk)
        v = _split_heads(y @ Wv + bv)
        scale = 1.0 / math.sqrt(D_HEAD)
        scores = jnp.einsum('bhqd,bhkd->bhqk', q, k) * scale
        weights = jax.nn.softmax(scores, axis=-1)
        out = jnp.einsum('bhqk,bhkd->bhqd', weights, v)
        out = out.transpose(0, 2, 1, 3).reshape(x.shape[0], x.shape[1], D_ATT)
        return out @ Wo + bo

    def _L0_ffn_ref(hidden_states, gate_w, gate_bias, eg_w, eu_w, ed_w, sg_w, su_w, sd_w):
        import jax, jax.numpy as jnp
        import numpy as np
        from jax import lax
        HIDDEN = 128
        INTER = 64
        E = 64
        K = 6
        G = 8
        TG = 4
        NSH = 2
        ISH = INTER * NSH

        def _moe_forward(hidden_states, gate_w, gate_bias, eg_w, eu_w, ed_w, sg_w, su_w, sd_w):
            B, S, H = hidden_states.shape
            x = hidden_states.reshape(-1, H)
            T = x.shape[0]
            shared = jax.nn.silu(x @ sg_w.T) * (x @ su_w.T) @ sd_w.T
            logits = x @ gate_w.T
            scores = jax.nn.sigmoid(logits) + gate_bias
            group_scores = scores.reshape(T, G, E // G).max(axis=-1)
            _, sel_groups = lax.top_k(group_scores, TG)
            group_mask = jnp.zeros((T, G), scores.dtype).at[jnp.arange(T)[:, None], sel_groups].set(1.0)
            mask = jnp.repeat(group_mask, E // G, axis=1)
            masked_scores = scores * mask
            topk_w, topk_i = lax.top_k(masked_scores, K)
            topk_w = topk_w / (topk_w.sum(axis=-1, keepdims=True) + 1e-08)
            comb = jnp.zeros((T, E), x.dtype).at[jnp.arange(T)[:, None], topk_i].add(topk_w)
            h = jax.nn.silu(jnp.einsum('th,eih->eti', x, eg_w)) * jnp.einsum('th,eih->eti', x, eu_w)
            routed = jnp.einsum('eti,ehi,te->th', h, ed_w, comb)
            return (shared + routed).reshape(B, S, H)
        return _moe_forward(hidden_states, gate_w, gate_bias, eg_w, eu_w, ed_w, sg_w, su_w, sd_w)
    x = x + _L0_xattn_ref(_layernorm(x, axis=-1), ctx_768, L0_xattn_Wq, L0_xattn_bq, L0_xattn_Wk, L0_xattn_bk, L0_xattn_Wv, L0_xattn_bv, L0_xattn_Wo, L0_xattn_bo)
    x = x + _L0_ffn_ref(_layernorm(x, axis=-1), L0_ffn_gate_w, L0_ffn_gate_bias, L0_ffn_eg_w, L0_ffn_eu_w, L0_ffn_ed_w, L0_ffn_sg_w, L0_ffn_su_w, L0_ffn_sd_w)
    return x

_drawn_inputs = setup_inputs


def setup_inputs(seed=0):
    import zlib

    import numpy as np

    out = dict(_drawn_inputs(seed))
    spreads = {'L0_ffn_gate_bias': (0.0, 0.8)}
    factors = {'L0_xattn_bq': 8.0,
     'L0_xattn_bk': 8.0,
     'L0_xattn_bv': 6.351,
     'L0_xattn_bo': 5.77,
     'L0_ffn_gate_w': 8.0,
     'L0_ffn_eg_w': 8.0,
     'L0_ffn_eu_w': 8.0,
     'L0_ffn_ed_w': 8.0,
     'L0_ffn_sg_w': 8.0,
     'L0_ffn_su_w': 8.0,
     'L0_ffn_sd_w': 8.0}
    for name, (base, spread) in spreads.items():
        noise = np.random.default_rng([zlib.crc32(name.encode()), seed]).standard_normal(out[name].shape)
        drawn = base * np.exp(spread * noise) if base else spread * noise
        out[name] = jnp.asarray(drawn.astype(out[name].dtype))
    for name, factor in factors.items():
        out[name] = (out[name] * factor).astype(out[name].dtype)
    return out
```

```python
from contextlib import ExitStack

import numpy as np

import concourse.bass as bass
from concourse import mybir

F32 = mybir.dt.float32
F32R = mybir.dt.float32r
ALU = mybir.AluOpType
ACT = mybir.ActivationFunctionType
AX = mybir.AxisListType

P = 128
B = 16
TPB = 2
TOK = TPB * P
KV = 64
D = 128
DC = 96
NH = 16
DH = D // NH
HP = NH // 2
VW = 2 * (DH + 1)
E = 64
INTER = 64
G = 8
TG = 4
TOPK = 6
NPAIR = E // 2
NSTEP = NPAIR + 1
SHARED = NPAIR
CH = 512
NCH = B * TOK // CH
SCALE = 1.0 / float(np.sqrt(DH))
EPS = 1e-5
BIG = 3.0e38
TAKEN = -1.0e38
ROUTE_STEPS = 21


def build(nc, x, ctx_rows, wq, bq, wk, bk, wv, bv, wo, bo, gate_w, gate_bias, eg, eu, ed, sg, su, sd, out):
    with ExitStack() as ctx:
        def sb(name, shape, dt=F32):
            return ctx.enter_context(nc.sbuf_tensor(name, shape, dt))

        def ps(name, cols):
            return ctx.enter_context(nc.psum_tensor(name, [P, cols], F32))

        def sem(name):
            return ctx.enter_context(nc.semaphore(name))

        bank_s = [ps(f"bank_s{j}", 1024) for j in range(TPB)]
        bank_q = ps("bank_q", 512)
        bank_o = ps("bank_o", 512)
        bank_r = ps("bank_r", 512)
        bank_w = ps("bank_w", 512)
        g_ps = [bank_s[0][:, i * CH:(i + 1) * CH] for i in range(2)]
        u_ps = [bank_s[1][:, i * CH:(i + 1) * CH] for i in range(2)]
        c_ps = [bank_q, bank_o]

        w_hi = sb("w_hi", [P, NSTEP, 3, P], F32R)
        w_lo = sb("w_lo", [P, NSTEP, 3, P], F32R)
        xh = sb("xh", [P, B * TOK], F32R)
        xl = sb("xl", [P, B * TOK], F32R)
        comb_t = sb("comb_t", [P, B * TOK], F32R)
        xb = sb("xb", [P, B * TPB, D])
        ident = sb("ident", [P, P])
        pick = sb("pick", [P, E])
        head_mask = sb("head_mask", [P, NH])
        wq_s = sb("wq_s", [D, D])
        wk_s = sb("wk_s", [DC, D])
        wv_s = sb("wv_s", [DC, D])
        wo_s = sb("wo_s", [D, D])
        bq_s = sb("bq_s", [D, 1])
        bk_s = sb("bk_s", [D, 1])
        bv_s = sb("bv_s", [P, D])
        bo_s = sb("bo_s", [P, D])
        gw_t = sb("gw_t", [D, E])
        gb_s = sb("gb_s", [P, E])
        eps_s = sb("eps_s", [P, TPB])
        minus_half = sb("minus_half", [P, TPB])
        ctx_s = sb("ctx_s", [P, DC])
        raw_w = sb("raw_w", [P, 6, P])
        st1 = sb("st1", [P, TPB, 6])
        mv1 = sb("mv1", [P, TPB, 2])
        ve1 = sb("ve1", [P, TPB])
        rstd1 = sb("rstd1", [P, TPB])
        st2 = sb("st2", [P, TPB, 6])
        mv2 = sb("mv2", [P, TPB, 2])
        ve2 = sb("ve2", [P, TPB])
        rstd2 = sb("rstd2", [P, TPB])
        xn = sb("xn", [P, TPB, D])
        xn_t = sb("xn_t", [P, TOK])
        q_t = sb("q_t", [P, TOK])
        k_t = sb("k_t", [P, KV])
        k_exp = sb("k_exp", [P, NH, KV])
        v_s = sb("v_s", [P, D])
        ctx_t = v_s[0:DC, :]
        v_blk = sb("v_blk", [P, HP, VW])
        mx = sb("mx", [P, TPB, NH])
        p_s = sb("p_s", [P, TPB, NH * KV])
        p_t = sb("p_t", [P, HP * P])
        rsum = sb("rsum", [P, TPB * NH])
        o_s = xn[:, :, :].rearrange("p t (h d) -> p (t h) d", d=DH)
        o_t = xn_t
        xn2 = sb("xn2", [P, TPB, D])
        gw_raw = xn2[0:E, 0, :]
        x2_t = sb("x2_t", [P, TOK])
        sig_score = sb("sig_score", [P, 2, TPB, E])
        sig = sig_score[:, 0]
        score = sig_score[:, 1]
        grp = sb("grp", [P, TPB, G + 4])
        grp_top = sb("grp_top", [P, TPB, 8])
        grp_rep = sb("grp_rep", [P, TPB, G + 4])
        msk = sb("msk", [P, TPB, E + 2])
        top = sb("top", [P, TPB, 8])
        msk_rep = sig_score[:, :, :, :].rearrange("p a t e -> p (a t e)")[:, 0:TPB * (E + 2)].rearrange(
            "p (t e) -> p t e", t=TPB)
        wsum = sb("wsum", [P, TPB])
        comb = msk[:, :, 0:E]
        comb2 = xn2[:, :, :].rearrange("p t (a e) -> p t a e", a=2)
        s_act = p_s[:, 0, 0:CH]
        h_s = [p_s[:, 0, CH:2 * CH], p_s[:, 1, 0:CH], p_s[:, 1, CH:2 * CH]]
        sum_s = p_t[:, 0:CH]
        y_s = p_t[:, CH:2 * CH]
        h_hi = sb("h_hi", [P, 3, CH], F32R)
        h_lo = sb("h_lo", [P, 2, CH], F32R)
        sel = sb("sel", [P, 3, 2, INTER], F32R)

        x_first, x_rest, const_in, gate_in = sem("x_first"), sem("x_rest"), sem("const_in"), sem("gate_in")
        ctx_in, raw_in = sem("ctx_in"), sem("raw_in")
        zeroed, made, filled = sem("zeroed"), sem("made"), sem("filled")
        gwt_done, gwt_ready = sem("gwt_done"), sem("gwt_ready")
        st1_done, mv1_done, ve1_done, rstd1_done = sem("st1_done"), sem("mv1_done"), sem("ve1_done"), sem("rstd1_done")
        st2_done, mv2_done, ve2_done, rstd2_done = sem("st2_done"), sem("mv2_done"), sem("ve2_done"), sem("rstd2_done")
        xn_ready, xb_ready, xt_done, xts_ready = sem("xn_ready"), sem("xb_ready"), sem("xt_done"), sem("xts_ready")
        qkv_done, q_ready, k_ready, v_ready = sem("qkv_done"), sem("q_ready"), sem("k_ready"), sem("v_ready")
        kexp_ready, vblk_ready = sem("kexp_ready"), sem("vblk_ready")
        scores_done, mx_done, shifted, p_ready = sem("scores_done"), sem("mx_done"), sem("shifted"), sem("p_ready")
        pt_done, pt_ready, pv_done = sem("pt_done"), sem("pt_ready"), sem("pv_done")
        rsum_done, o_ready, ot_done, ot_ready = sem("rsum_done"), sem("o_ready"), sem("ot_done"), sem("ot_ready")
        wo_done, x2_done = sem("wo_done"), sem("x2_done")
        xn2_ready, x2t_done, x2t_ready = sem("xn2_ready"), sem("x2t_done"), sem("x2t_ready")
        xh_ready, xl_ready = sem("xh_ready"), sem("xl_ready")
        logit_done, sig_ready, route = sem("logit_done"), sem("sig_ready"), sem("route")
        combt_done, combt_ready = sem("combt_done"), sem("combt_ready")
        wa_done, wa_hi, wa_lo = sem("wa_done"), sem("wa_hi"), sem("wa_lo")
        wb_done, wb_hi, wb_lo = sem("wb_done"), sem("wb_hi"), sem("wb_lo")
        sel_ready = sem("sel_ready")
        gu_done, s_ready, t_done, h_done = sem("gu_done"), sem("s_ready"), sem("t_done"), sem("h_done")
        hi_ready, lo_ready, down_done = sem("hi_ready"), sem("lo_ready"), sem("down_done")
        sum_ready, sumt_done, y_ready, y_out = sem("sum_ready"), sem("sumt_done"), sem("y_ready"), sem("y_out")

        x_v = x.rearrange("b (t p) h -> p (b t) h", p=P)
        out_v = out.rearrange("b (t p) h -> p (b t) h", p=P)
        eg_v = eg.rearrange("(w j a) i h -> w (a i) j h", j=2, a=2)
        eu_v = eu.rearrange("(w j a) i h -> w (a i) j h", j=2, a=2)
        ed_v = ed.rearrange("(w e) h i -> w h e i", e=4)
        NCONST = 9

        def row(ap):
            return ap.rearrange("(a n) -> a n", a=1)

        def col(ap):
            return ap.rearrange("(p a) -> p a", a=1)

        def phase1(eng, prologue, body, epilogue):
            prologue()
            body(0, True, False)
            body(1, True, True)
            with eng.Fori(2, B - 1) as b:
                body(b, True, True)
            body(B - 1, False, True)
            epilogue()

        block = ctx.enter_context(nc.Block())

        @block.sync
        def _(sp):
            def load_ctx(b):
                for half in range(2):
                    sp.dma_start(ctx_s[half * KV:(half + 1) * KV, :], ctx_rows[bass.ds(b, 1), :, :].rearrange(
                        "a s d -> (a s) d")).then_inc(ctx_in, 16)

            def load_raw(w):
                sp.dma_start(raw_w[:, 0:2, :], eg_v[bass.ds(w, 1), :, :, :].rearrange(
                    "a p j h -> (a p) j h")).then_inc(raw_in, 16)
                sp.dma_start(raw_w[:, 2:4, :], eu_v[bass.ds(w, 1), :, :, :].rearrange(
                    "a p j h -> (a p) j h")).then_inc(raw_in, 16)
                sp.dma_start(raw_w[:, 4:6, :].rearrange("p j (e i) -> p (j e) i", e=2), ed_v[
                    bass.ds(w, 1), :, :, :].rearrange("a h e i -> (a h) e i")).then_inc(raw_in, 16)

            sp.dma_start(xb[:, 0:TPB, :], x_v[:, 0:TPB, :]).then_inc(x_first, 16)
            load_ctx(0)
            for dst, src in ((wq_s, wq), (wk_s, wk), (wv_s, wv), (bq_s, col(bq)), (bk_s, col(bk)), (wo_s, wo)):
                sp.dma_start(dst[:, :], src).then_inc(const_in, 16)
            for dst, src, n in ((bv_s, bv, D), (bo_s, bo, D), (gb_s, gate_bias, E)):
                sp.dma_start(dst[:, :], row(src).to_broadcast([P, n])).then_inc(const_in, 16)
            sp.dma_start(gw_raw, gate_w).then_inc(gate_in, 16)
            sp.dma_start(raw_w[:, 0, :], sg).then_inc(raw_in, 16)
            sp.dma_start(raw_w[:, 2, :], su).then_inc(raw_in, 16)
            sp.dma_start(raw_w[:, 4, :], sd).then_inc(raw_in, 16)
            sp.dma_start(xb[:, TPB:, :], x_v[:, TPB:, :]).then_inc(x_rest, 16)
            with sp.Fori(0, B - 1) as b:
                sp.wait_ge(xt_done, b + 1)
                load_ctx(b + 1)
                sp.wait_ge(wb_done, b + 1)
                load_raw(b)
            sp.wait_ge(wb_done, B)
            load_raw(B - 1)
            with sp.Fori(0, NCH) as c:
                sp.wait_ge(y_ready, c + 1)
                sp.dma_start(out_v[:, bass.ds(c * 4, 4), :], y_s.rearrange("p (t h) -> p t h", h=D)).then_inc(y_out, 16)
            sp.wait_ge(y_out, 16 * NCH)

        @block.gpsimd
        def _(pool):
            for t in (ident[:, :], pick[:, :], v_blk[:, :, :]):
                pool.memset(t, 0.0).then_inc(zeroed, 1)
            pool.memset(head_mask[:, :], 1.0).then_inc(zeroed, 1)
            pool.memset(eps_s[:, :], EPS).then_inc(made, 1)
            pool.memset(minus_half[:, :], -0.5).then_inc(made, 1)
            pool.memset(grp[:, :, G:], BIG).then_inc(made, 1)
            pool.memset(msk[:, :, E:], BIG).then_inc(made, 1)
            pool.wait_ge(zeroed, 4)
            pool.affine_select(out=ident[:, :], in_=ident[:, :], compare_op=ALU.not_equal, fill=1.0, base=0,
                               pattern=[[-1, P]], channel_multiplier=1).then_inc(made, 1)
            pool.affine_select(out=pick[:, :], in_=pick[:, :], compare_op=ALU.not_equal, fill=1.0, base=0,
                               pattern=[[-1, E]], channel_multiplier=1).then_inc(filled, 1)
            pool.affine_select(out=head_mask[:, :], in_=head_mask[:, :], compare_op=ALU.is_ge, fill=0.0, base=0,
                               pattern=[[-DH, NH]], channel_multiplier=1).then_inc(filled, 1)
            pool.wait_ge(filled, 2)
            pool.affine_select(out=pick[:, :], in_=pick[:, :], compare_op=ALU.not_equal, fill=1.0, base=-E,
                               pattern=[[-1, E]], channel_multiplier=1).then_inc(made, 1)
            pool.affine_select(out=head_mask[:, :], in_=head_mask[:, :], compare_op=ALU.is_ge, fill=0.0, base=DH - 1,
                               pattern=[[DH, NH]], channel_multiplier=-1).then_inc(made, 1)
            pool.wait_ge(made, 7)

            def rstd(n, mv_done, ve_done, rstd_done, mv, ve, r):
                pool.wait_ge(mv_done, TPB * (n + 1))
                pool.tensor_tensor(ve[:, :], mv[:, :, 1], eps_s[:, :], ALU.add).then_inc(ve_done, 1)
                pool.wait_ge(ve_done, n + 1)
                pool.tensor_tensor(r[:, :], ve[:, :], minus_half[:, :], ALU.pow).then_inc(rstd_done, 1)

            def add_bo(n):
                pool.wait_ge(xn_ready, TPB * (n + 1))
                for t in range(TPB):
                    xt = xb[:, bass.ds(TPB * n + t, 1), :].rearrange("p t h -> p (t h)")
                    pool.tensor_tensor(xt, xt, bo_s[:, :], ALU.add).then_inc(xb_ready, 1)

            def expand_k(n):
                pool.wait_ge(k_ready, n + 1)
                pool.tensor_tensor(k_exp[:, :, :], k_t[:, :].unsqueeze(1).to_broadcast([P, NH, KV]),
                                   head_mask[:, :].unsqueeze(2).to_broadcast([P, NH, KV]),
                                   ALU.mult).then_inc(kexp_ready, 1)

            def split_x(n):
                pool.wait_ge(xh_ready, n + 1)
                cols = bass.ds(n * TOK, TOK)
                pool.tensor_tensor(xl[:, cols], x2_t[:, :], xh[:, cols].bitcast(F32), ALU.subtract).then_inc(xl_ready, 1)

            def norm1(n):
                rstd(n, mv1_done, ve1_done, rstd1_done, mv1, ve1, rstd1)

            def norm2(n):
                rstd(n, mv2_done, ve2_done, rstd2_done, mv2, ve2, rstd2)

            def prologue():
                norm1(0)
                pool.wait_ge(const_in, 16 * NCONST)
                add_bo(0)
                expand_k(0)

            def body(b, nxt, prv):
                if prv:
                    norm2(b - 1)
                if nxt:
                    norm1(b + 1)
                    add_bo(b + 1)
                if prv:
                    split_x(b - 1)
                if nxt:
                    expand_k(b + 1)

            def epilogue():
                norm2(B - 1)
                split_x(B - 1)

            phase1(pool, prologue, body, epilogue)

            def selector(k):
                pair = min(k, NPAIR - 1)
                two = pick[:, 2 * pair:2 * pair + 2].unsqueeze(2).to_broadcast([P, 2, INTER])
                pool.tensor_tensor(sel[:, k % 3, :, :], two, two, ALU.mult).then_inc(sel_ready, 1)

            for k in range(3):
                selector(k)
            def chunk(c):
                for k in range(NSTEP):
                    n = c * NSTEP + k
                    pool.wait_ge(gu_done, n + 1)
                    selector((k + 3) % NSTEP)
                    pool.wait_ge(hi_ready, n + 1)
                    pool.wait_ge(down_done, n if k == 0 else n - 1)
                    pool.tensor_tensor(h_lo[:, k % 2, :], h_s[k % 3], h_hi[:, k % 3, :].bitcast(F32),
                                       ALU.subtract).then_inc(lo_ready, 1)

            chunk(0)
            with pool.Fori(1, NCH) as c:
                chunk(c)

        @block.scalar
        def _(act):
            def copy(dst, src):
                return act.activation(dst, src, ACT.Copy)

            def weights_hi(done, ready, w, dst, src):
                act.wait_ge(done, w + 1)
                copy(dst, src).then_inc(ready, 1)

            def transposed_x(n):
                act.wait_ge(xt_done, n + 1)
                copy(xn_t[:, :], bank_q[:, 0:TOK]).then_inc(xts_ready, 1)
                copy(ctx_t, bank_q[0:DC, TOK:TOK + P]).then_inc(xts_ready, 1)

            def transposed_x2(n):
                act.wait_ge(xl_ready, n)
                act.wait_ge(x2t_done, n + 1)
                copy(x2_t[:, :], bank_r[:, 0:TOK]).then_inc(x2t_ready, 1)

            def exps(b, j):
                act.wait_ge(shifted, TPB * b + j + 1)
                act.activation(p_s[:, j, :], p_s[:, j, :], ACT.Exp).then_inc(p_ready, 1)

            def copy_pt(b, j):
                act.wait_ge(pt_done, TPB * b + j + 1)
                copy(p_t[:, :], bank_s[j][:, :]).then_inc(pt_ready, 1)

            def sigmoid_exp(n):
                act.wait_ge(logit_done, n + 1)
                act.activation(sig[:, :, :].rearrange("p t e -> p (t e)"), bank_r[:, TOK:TOK + TPB * E], ACT.Exp,
                               scale=-1.0).then_inc(sig_ready, 1)

            def copy_comb(n):
                act.wait_ge(combt_done, n + 1)
                copy(comb_t[:, bass.ds(n * TOK, TOK)], bank_r[:, 0:TOK]).then_inc(combt_ready, 1)

            def prologue():
                act.wait_ge(gwt_done, 1)
                copy(gw_t[:, :], bank_r[:, 0:E]).then_inc(gwt_ready, 1)
                transposed_x(0)
                weights_hi(wa_done, wa_hi, 0, w_hi[:, SHARED, 0:2, :], bank_w[:, 0:2 * P])
                weights_hi(wb_done, wb_hi, 0, w_hi[:, SHARED, 2, :], bank_w[:, 0:P])

            def body(b, nxt, prv):
                exps(b, 0)
                if nxt:
                    transposed_x(b + 1)
                if prv:
                    transposed_x2(b - 1)
                exps(b, 1)
                weights_hi(wa_done, wa_hi, b + 1, w_hi[:, bass.ds(2 * b, 2), 0:2, :].rearrange("p j a h -> p j (a h)"),
                           bank_w[:, :].rearrange("p (j c) -> p j c", j=2))
                copy_pt(b, 0)
                if prv:
                    sigmoid_exp(b - 1)
                copy_pt(b, 1)
                weights_hi(wb_done, wb_hi, b + 1, w_hi[:, bass.ds(2 * b, 2), 2, :],
                           bank_w[:, 0:2 * P].rearrange("p (j c) -> p j c", j=2))
                if prv:
                    copy_comb(b - 1)
                act.wait_ge(ot_done, b + 1)
                copy(o_t[:, :], bank_o[:, 0:TOK]).then_inc(ot_ready, 1)

            def epilogue():
                transposed_x2(B - 1)
                sigmoid_exp(B - 1)
                copy_comb(B - 1)

            phase1(act, prologue, body, epilogue)

            def chunk(c):
                for k in range(NSTEP):
                    n = c * NSTEP + k
                    act.wait_ge(gu_done, n + 1)
                    act.wait_ge(t_done, n)
                    act.activation(s_act, g_ps[k % 2], ACT.Silu).then_inc(s_ready, 1)
                act.wait_ge(down_done, c * NSTEP + NSTEP)
                copy(sum_s, bank_r[:, :]).then_inc(sum_ready, 1)

            chunk(0)
            with act.Fori(1, NCH) as c:
                chunk(c)

        @block.vector
        def _(dve):
            dve.wait_ge(made, 7)
            dve.memset(v_blk[0:KV, :, DH:DH + 1], 1.0)
            dve.memset(v_blk[KV:P, :, VW - 1:VW], 1.0)

            def x_tile(i):
                return xb[:, bass.ds(i, 1), :].rearrange("p t h -> p (t h)")

            def stats(n, st, st_done):
                for t in range(TPB):
                    dve.bn_stats(st[:, t, :], x_tile(TPB * n + t)).then_inc(st_done, 1)

            def aggregate(st, mv, mv_done):
                for t in range(TPB):
                    dve.bn_aggr(mv[:, t, :], st[:, t, :]).then_inc(mv_done, 1)

            def normalize(n, dst, mv, r, r_done, ready):
                dve.wait_ge(r_done, n + 1)
                for t in range(TPB):
                    dve.tensor_scalar(dst[:, t, :], x_tile(TPB * n + t), mv[:, t, 0:1], r[:, t:t + 1],
                                      ALU.subtract, ALU.mult).then_inc(ready, 1)


            def shift(b, j, between=()):
                s = bank_s[j][:, :].rearrange("p (h k) -> p h k", k=KV)
                dve.wait_ge(scores_done, TPB * b + j + 1)
                dve.tensor_reduce(mx[:, j, :], s, AX.X, ALU.max).then_inc(mx_done, 1)
                for step in between:
                    step()
                dve.wait_ge(mx_done, TPB * b + j + 1)
                dve.tensor_tensor(p_s[:, j, :].rearrange("p (h k) -> p h k", k=KV), s,
                                  mx[:, j, :].unsqueeze(2).to_broadcast([P, NH, KV]), ALU.subtract).then_inc(shifted, 1)

            def evacuate_q(n):
                dve.wait_ge(qkv_done, n + 1)
                dve.tensor_scalar(q_t[:, :], bank_q[:, 0:TOK], bq_s[:, 0:1], SCALE, ALU.add, ALU.mult).then_inc(q_ready, 1)

            def evacuate_k(n):
                dve.tensor_scalar(k_t[:, :], bank_q[:, TOK:TOK + KV], bk_s[:, 0:1], None, ALU.add).then_inc(k_ready, 1)

            def evacuate_v(n):
                dve.tensor_tensor(v_s[:, :], bank_q[:, TOK + KV:TOK + KV + D], bv_s[:, :], ALU.add).then_inc(v_ready, 1)

            def v_blocks(n):
                dve.wait_ge(v_ready, n + 1)
                for h in range(2):
                    rows = slice(h * KV, (h + 1) * KV)
                    dve.tensor_copy(v_blk[rows, :, h * (DH + 1):h * (DH + 1) + DH],
                                    v_s[rows, :].rearrange("p (a h d) -> p a h d", h=2, d=DH)[:, :, h, :]).then_inc(vblk_ready, 1)

            def weights_lo(ready, done, w, dst, src, hi):
                dve.wait_ge(ready, w + 1)
                dve.tensor_tensor(dst, src, hi.bitcast(F32), ALU.subtract).then_inc(done, 1)

            def two(t, b, part):
                v = t[:, bass.ds(2 * b, 2), part, :]
                return v.rearrange("p j a h -> p j (a h)") if isinstance(part, slice) else v

            def routing(n, between=()):
                at = [0]
                between = list(between)

                def settle_between():
                    settle()
                    if between:
                        between.pop(0)()

                def chained(ins):
                    at[0] += 1
                    ins.then_inc(route, 1)

                def settle():
                    dve.wait_ge(route, n * ROUTE_STEPS + at[0])

                flat = lambda t: t[:, :, :].rearrange("p t e -> p (t e)")
                dve.wait_ge(sig_ready, n + 1)
                chained(dve.tensor_scalar(flat(sig), flat(sig), 1.0, None, ALU.add))
                settle()
                chained(dve.reciprocal(flat(score), flat(sig)))
                settle()
                chained(dve.tensor_tensor(score[:, :, :], score[:, :, :], gb_s[:, :].unsqueeze(1).to_broadcast([P, TPB, E]), ALU.add))
                settle()
                chained(dve.tensor_reduce(grp[:, :, 0:G], score[:, :, :].rearrange("p t (g e) -> p t g e", g=G), AX.X, ALU.max))
                settle_between()
                for t in range(TPB):
                    chained(dve.max(grp_top[:, t, :], grp[:, t, :]))
                settle_between()
                for t in range(TPB):
                    chained(dve.match_replace(grp_rep[:, t, :], grp_top[:, t, :], grp[:, t, :], -BIG))
                settle()
                for t in range(TPB):
                    chained(dve.scalar_tensor_tensor(
                        out=msk[:, t, 0:E].rearrange("p (g e) -> p g e", g=G),
                        in0=grp_rep[:, t, 0:G].unsqueeze(2).to_broadcast([P, G, E // G]), scalar=TAKEN,
                        in1=score[:, t, :].rearrange("p (g e) -> p g e", g=G), op0=ALU.is_lt, op1=ALU.mult))
                settle_between()
                for t in range(TPB):
                    chained(dve.max(top[:, t, :], msk[:, t, :]))
                settle_between()
                for t in range(TPB):
                    chained(dve.match_replace(msk_rep[:, t, :], top[:, t, :], msk[:, t, :], -BIG))
                chained(dve.tensor_reduce(wsum[:, :], top[:, :, 8 - TOPK:8], AX.X, ALU.add))
                settle()
                chained(dve.scalar_tensor_tensor(out=comb[:, :, :], in0=msk_rep[:, :, 0:E], scalar=TAKEN,
                                                 in1=msk[:, :, 0:E], op0=ALU.is_lt, op1=ALU.mult))
                chained(dve.tensor_scalar(wsum[:, :], wsum[:, :], 1e-8, None, ALU.add))
                settle()
                chained(dve.reciprocal(wsum[:, :], wsum[:, :]))
                settle()
                chained(dve.tensor_tensor(comb[:, :, :], comb[:, :, :], wsum[:, :].unsqueeze(2).to_broadcast([P, TPB, E]), ALU.mult))
                settle()
                chained(dve.tensor_copy(comb2[:, :, 0, :].bitcast(F32R), comb[:, :, :]))
                settle()
                chained(dve.tensor_tensor(comb2[:, :, 1, :], comb[:, :, :], comb2[:, :, 0, :], ALU.subtract))
                assert at[0] == ROUTE_STEPS

            def split_hi(n):
                dve.wait_ge(x2t_ready, n + 1)
                dve.tensor_copy(xh[:, bass.ds(n * TOK, TOK)], x2_t[:, :]).then_inc(xh_ready, 1)

            def prologue():
                dve.wait_ge(x_first, 16)
                stats(0, st1, st1_done)
                dve.wait_ge(st1_done, TPB)
                aggregate(st1, mv1, mv1_done)
                normalize(0, xn, mv1, rstd1, rstd1_done, xn_ready)
                dve.wait_ge(const_in, 16 * NCONST)
                evacuate_q(0)
                evacuate_k(0)
                evacuate_v(0)
                v_blocks(0)
                weights_lo(wa_hi, wa_lo, 0, w_lo[:, SHARED, 0:2, :].rearrange("p a h -> p (a h)"), bank_w[:, 0:2 * P],
                           w_hi[:, SHARED, 0:2, :].rearrange("p a h -> p (a h)"))
                weights_lo(wb_hi, wb_lo, 0, w_lo[:, SHARED, 2, :], bank_w[:, 0:P], w_hi[:, SHARED, 2, :])
                dve.wait_ge(x_rest, 16)

            def body(b, nxt, prv):
                if prv:
                    dve.wait_ge(x2_done, b)
                    stats(b - 1, st2, st2_done)
                if nxt:
                    stats(b + 1, st1, st1_done)
                if prv:
                    dve.wait_ge(st2_done, TPB * b)
                if nxt:
                    dve.wait_ge(st1_done, TPB * (b + 2))
                shift(b, 0, ([lambda: aggregate(st2, mv2, mv2_done)] if prv else [])
                      + ([lambda: aggregate(st1, mv1, mv1_done)] if nxt else []))
                if nxt:
                    normalize(b + 1, xn, mv1, rstd1, rstd1_done, xn_ready)
                if prv:
                    normalize(b - 1, xn2, mv2, rstd2, rstd2_done, xn2_ready)
                if prv:
                    split_hi(b - 1)
                shift(b, 1)
                def split_a():
                    weights_lo(wa_hi, wa_lo, b + 1, two(w_lo, b, slice(0, 2)),
                               bank_w[:, :].rearrange("p (j c) -> p j c", j=2), two(w_hi, b, slice(0, 2)))

                between = [split_a]
                if nxt:
                    between += [lambda: evacuate_q(b + 1), lambda: evacuate_k(b + 1), lambda: evacuate_v(b + 1)]
                if prv and nxt:
                    routing(b - 1, between)
                else:
                    for step in between:
                        step()
                    if prv:
                        routing(b - 1)
                weights_lo(wb_hi, wb_lo, b + 1, two(w_lo, b, 2), bank_w[:, 0:2 * P].rearrange("p (j c) -> p j c", j=2),
                           two(w_hi, b, 2))
                pv = bank_o[:, 0:TPB * HP * VW].rearrange("p (h e) -> p h e", e=DH + 1)
                dve.wait_ge(pv_done, b + 1)
                dve.reciprocal(rsum[:, :], pv[:, :, DH]).then_inc(rsum_done, 1)
                dve.wait_ge(rsum_done, b + 1)
                dve.tensor_tensor(o_s[:, :, :], pv[:, :, 0:DH], rsum[:, :].unsqueeze(2).to_broadcast([P, TPB * NH, DH]),
                                  ALU.mult).then_inc(o_ready, 1)
                if nxt:
                    v_blocks(b + 1)
                dve.wait_ge(wo_done, b + 1)
                dve.wait_ge(xb_ready, TPB * (b + 1))
                xt = xb[:, bass.ds(TPB * b, TPB), :]
                dve.tensor_tensor(xt, bank_o[:, TOK:2 * TOK].rearrange("p (t h) -> p t h", h=D), xt, ALU.add).then_inc(x2_done, 1)

            def epilogue():
                dve.wait_ge(x2_done, B)
                stats(B - 1, st2, st2_done)
                dve.wait_ge(st2_done, TPB * B)
                aggregate(st2, mv2, mv2_done)
                normalize(B - 1, xn2, mv2, rstd2, rstd2_done, xn2_ready)
                split_hi(B - 1)
                routing(B - 1)

            phase1(dve, prologue, body, epilogue)

            def chunk(c, first):
                for k in range(NSTEP):
                    n = c * NSTEP + k
                    dve.wait_ge(s_ready, n + 1)
                    if k >= 3 or not first:
                        dve.wait_ge(lo_ready, n - 2)
                    dve.tensor_tensor(h_s[k % 3], u_ps[k % 2], s_act, ALU.mult).then_inc(t_done, 1)
                    dve.wait_ge(t_done, n + 1)
                    if k != SHARED:
                        dve.tensor_tensor(h_s[k % 3], c_ps[k % 2][:, :], h_s[k % 3], ALU.mult).then_inc(h_done, 1)
                        dve.wait_ge(h_done, c * NPAIR + k + 1)
                    if k >= 3 or not first:
                        dve.wait_ge(down_done, n - 2)
                    dve.tensor_copy(h_hi[:, k % 3, :], h_s[k % 3]).then_inc(hi_ready, 1)
                dve.wait_ge(sumt_done, c + 1)
                dve.wait_ge(y_out, 16 * c)
                xt = xb[:, bass.ds(4 * c, 4), :]
                dve.tensor_tensor(y_s.rearrange("p (t h) -> p t h", h=D), bank_w[:, :].rearrange("p (t h) -> p t h", h=D),
                                  xt, ALU.add).then_inc(y_ready, 1)

            chunk(0, True)
            with dve.Fori(1, NCH) as c:
                chunk(c, False)

        @block.tensor
        def _(pe):
            def transposes(outs, ins, done):
                for o, i in zip(outs, ins):
                    k = i.shape[0]
                    last = pe.transpose(o, i, ident[0:k, 0:k])
                last.then_inc(done, 1)

            def mm(dst, w, v):
                return pe.matmul(dst, w, v, start=True, stop=True)

            def transpose_x(n):
                pe.wait_ge(xn_ready, TPB * (n + 1))
                pe.wait_ge(ctx_in, 32 * (n + 1))
                pe.wait_ge(v_ready, n)
                transposes([bank_q[:, t * P:(t + 1) * P] for t in range(TPB)] + [bank_q[0:DC, TOK:TOK + P]],
                           [xn[:, t, :] for t in range(TPB)] + [ctx_s[:, :]], xt_done)

            def project(n):
                pe.wait_ge(xts_ready, 2 * (n + 1))
                mm(bank_q[:, 0:TOK], wq_s[:, :], xn_t[:, :])
                mm(bank_q[:, TOK:TOK + KV], wk_s[:, :], ctx_t[:, 0:KV])
                mm(bank_q[:, TOK + KV:TOK + KV + D], ctx_t, wv_s[:, :]).then_inc(qkv_done, 1)

            def transpose_x2(n):
                pe.wait_ge(xn2_ready, TPB * (n + 1))
                pe.wait_ge(combt_ready, n)
                transposes([bank_r[:, t * P:(t + 1) * P] for t in range(TPB)], [xn2[:, t, :] for t in range(TPB)], x2t_done)

            def logits(n):
                pe.wait_ge(x2t_ready, n + 1)
                for t in range(TPB):
                    last = mm(bank_r[:, TOK + t * E:TOK + (t + 1) * E], x2_t[:, t * P:(t + 1) * P], gw_t[:, :])
                last.then_inc(logit_done, 1)

            def transpose_comb(n):
                pe.wait_ge(route, ROUTE_STEPS * (n + 1))
                transposes([bank_r[:, t * P:(t + 1) * P] for t in range(TPB)],
                           [comb2[:, t, :, :].rearrange("p a e -> p (a e)") for t in range(TPB)], combt_done)

            def weights_a(w, slots):
                pe.wait_ge(raw_in, 48 * (w + 1))
                pe.wait_ge(wb_lo, w)
                transposes([bank_w[:, i * P:(i + 1) * P] for i in range(len(slots))], [raw_w[:, s, :] for s in slots], wa_done)

            def weights_b(w, slots):
                pe.wait_ge(wa_lo, w + 1)
                transposes([bank_w[:, i * P:(i + 1) * P] for i in range(len(slots))], [raw_w[:, s, :] for s in slots], wb_done)

            def scores(b, first):
                pe.wait_ge(q_ready, b + 1)
                pe.wait_ge(kexp_ready, b + 1)
                for j in range(TPB):
                    if not first:
                        pe.wait_ge(pt_ready, TPB * (b - 1) + j + 1)
                    for half in range(2):
                        last = mm(bank_s[j][:, half * 512:(half + 1) * 512], q_t[:, j * P:(j + 1) * P],
                                  k_exp[:, half * HP:(half + 1) * HP, :].rearrange("p h k -> p (h k)"))
                    last.then_inc(scores_done, 1)

            def transpose_p(b, j):
                pe.wait_ge(p_ready, TPB * b + j + 1)
                transposes([bank_s[j][:, a * P:(a + 1) * P] for a in range(HP)],
                           [p_s[:, j, a * P:(a + 1) * P] for a in range(HP)], pt_done)

            def values(b, j):
                pe.wait_ge(pt_ready, TPB * b + j + 1)
                for a in range(HP):
                    at = (j * HP + a) * VW
                    last = mm(bank_o[:, at:at + VW], p_t[:, a * P:(a + 1) * P], v_blk[:, a, :])
                return last

            def prologue():
                pe.wait_ge(made, 7)
                pe.wait_ge(gate_in, 16)
                transposes([bank_r[:, 0:E]], [gw_raw], gwt_done)
                transpose_x(0)
                weights_a(0, (0, 2))
                pe.wait_ge(const_in, 16 * NCONST)
                project(0)
                weights_b(0, (4,))
                pe.wait_ge(gwt_ready, 1)

            def body(b, nxt, prv):
                scores(b, not prv)
                if nxt:
                    transpose_x(b + 1)
                if prv:
                    transpose_x2(b - 1)
                weights_a(b + 1, (0, 2, 1, 3))
                transpose_p(b, 0)
                if nxt:
                    project(b + 1)
                if prv:
                    logits(b - 1)
                pe.wait_ge(vblk_ready, 2 * (b + 1))
                pe.wait_ge(x2_done, b)
                values(b, 0)
                transpose_p(b, 1)
                weights_b(b + 1, (4, 5))
                values(b, 1).then_inc(pv_done, 1)
                if prv:
                    transpose_comb(b - 1)
                pe.wait_ge(o_ready, b + 1)
                o_flat = o_s[:, :, :].rearrange("p h d -> p (h d)")
                transposes([bank_o[:, t * P:(t + 1) * P] for t in range(TPB)],
                           [o_flat[:, t * P:(t + 1) * P] for t in range(TPB)], ot_done)
                pe.wait_ge(ot_ready, b + 1)
                for t in range(TPB):
                    last = mm(bank_o[:, TOK + t * D:TOK + (t + 1) * D], o_t[:, t * P:(t + 1) * P], wo_s[:, :])
                last.then_inc(wo_done, 1)

            def epilogue():
                transpose_x2(B - 1)
                logits(B - 1)
                transpose_comb(B - 1)

            phase1(pe, prologue, body, epilogue)

            def three(dst, k, part, hi, lo, start=True, stop=True):
                pe.matmul(dst, w_hi[:, k, part, :], hi, start=start, stop=False)
                pe.matmul(dst, w_hi[:, k, part, :], lo, start=False, stop=False)
                return pe.matmul(dst, w_lo[:, k, part, :], hi, start=False, stop=stop)

            def gate_up(c, k, first):
                n = c * NSTEP + k
                cols = bass.ds(c * CH, CH)
                if k >= 2:
                    pe.wait_ge(hi_ready, n - 1)
                elif not first:
                    pe.wait_ge(hi_ready, n - k)
                last = three(g_ps[k % 2], k, 0, xh[:, cols], xl[:, cols])
                last = three(u_ps[k % 2], k, 1, xh[:, cols], xl[:, cols])
                if k != SHARED:
                    pe.wait_ge(sel_ready, c * NSTEP + k + 1)
                    last = pe.matmul(c_ps[k % 2][:, :], sel[:, k % 3, :, :].rearrange("p a i -> p (a i)"),
                                     comb_t[:, cols], start=True, stop=True)
                last.then_inc(gu_done, 1)

            def chunk(c, last_chunk):
                for k in range(NSTEP):
                    if k + 2 < NSTEP:
                        gate_up(c, k + 2, False)
                    elif not last_chunk:
                        gate_up(c + 1, k + 2 - NSTEP, False)
                    n = c * NSTEP + k
                    pe.wait_ge(lo_ready, n + 1)
                    if k == 0:
                        pe.wait_ge(sum_ready, c)
                    three(bank_r[:, :], k, 2, h_hi[:, k % 3, :], h_lo[:, k % 2, :], start=(k == 0),
                          stop=(k == SHARED)).then_inc(down_done, 1)
                pe.wait_ge(sum_ready, c + 1)
                pe.wait_ge(y_ready, c)
                transposes([bank_w[:, t * P:(t + 1) * P] for t in range(4)],
                           [sum_s[:, t * P:(t + 1) * P] for t in range(4)], sumt_done)

            pe.wait_ge(pt_ready, TPB * B)
            pe.wait_ge(x2_done, B)
            pe.wait_ge(combt_ready, B)
            pe.wait_ge(wb_lo, B + 1)
            pe.wait_ge(xl_ready, B)
            gate_up(0, 0, True)
            gate_up(0, 1, True)
            chunk(0, False)
            with pe.Fori(1, NCH - 1) as c:
                chunk(c, False)
            chunk(NCH - 1, True)


INPUTS = ["x", "ctx_768", "L0_xattn_Wq", "L0_xattn_bq", "L0_xattn_Wk", "L0_xattn_bk", "L0_xattn_Wv", "L0_xattn_bv",
          "L0_xattn_Wo", "L0_xattn_bo", "L0_ffn_gate_w", "L0_ffn_gate_bias", "L0_ffn_eg_w", "L0_ffn_eu_w",
          "L0_ffn_ed_w", "L0_ffn_sg_w", "L0_ffn_su_w", "L0_ffn_sd_w"]


def kernel(**inputs):
    import concourse.bacc as bacc
    from concourse.bass_utils import run_bass_kernel_spmd

    nc = bacc.Bacc("TRN2", target_bir_lowering=False, num_devices=1)
    arrays, args = {}, []
    for name in INPUTS:
        a = np.ascontiguousarray(inputs[name])
        arrays[f"in_{name}"] = a
        args.append(nc.dram_tensor(f"in_{name}", a.shape, mybir.dt.from_np(a.dtype), kind="ExternalInput").ap())
    args.append(nc.dram_tensor("out_x", (B, TOK, D), F32, kind="ExternalOutput").ap())
    build(nc, *args)
    return run_bass_kernel_spmd(nc, [arrays], core_ids=[0]).results[0]["out_x"]
```

```python
from contextlib import ExitStack

import numpy as np

import concourse.bass as bass
from concourse import mybir

F32 = mybir.dt.float32
BF16 = mybir.dt.bfloat16
I32 = mybir.dt.int32
U32 = mybir.dt.uint32
ALU = mybir.AluOpType
ACT = mybir.ActivationFunctionType
AX = mybir.AxisListType

P = 128
B = 16
TPB = 2
TOK = TPB * P
KV = 64
D = 128
DC = 96
NH = 16
DH = D // NH
HP = NH // 2
VW = 2 * (DH + 1)
E = 64
INTER = 64
G = 8
TG = 4
TOPK = 6
QUAD = 4
SLOTS = 4
PAGES = E + B * TOK * TOPK // P
NQ = PAGES // QUAD
CODE, EXPERT, WEIGHT = D, D + 1, D + 2
PC = D + 3
FILL = B * TOK * TOPK // P // B
FIRST_FILL = PAGES % FILL
FILLS_AHEAD = 1 + (E - FIRST_FILL) // FILL + 1
NO_CODE = 1000000
SCALE = 1.0 / float(np.sqrt(DH))
EPS = 1e-5
BIG = 3.0e38
TAKEN = -1.0e38
ROUTE_STEPS = 20
PLACE_STEPS = 22
NCONST = 9
MADE = 12


def build(nc, x, ctx_rows, wq, bq, wk, bk, wv, bv, wo, bo, gate_w, gate_bias, eg, eu, ed, sg, su, sd, out, pages, results):
    with ExitStack() as ctx:
        def sb(name, shape, dt=F32):
            return ctx.enter_context(nc.sbuf_tensor(name, shape, dt))

        def ps(name, cols):
            return ctx.enter_context(nc.psum_tensor(name, [P, cols], F32))

        def sem(name):
            return ctx.enter_context(nc.semaphore(name))

        bank_s = [ps(f"bank_s{j}", 1024) for j in range(TPB)]
        bank_q = ps("bank_q", 512)
        bank_o = ps("bank_o", 512)
        bank_r = ps("bank_r", 512)
        bank_w = ps("bank_w", 512)
        xt_ps = [bank_s[0][:, i * 512:(i + 1) * 512] for i in range(2)]
        gu_ps = [bank_s[1][:, i * 512:(i + 1) * 512] for i in range(2)]

        w_gu = sb("w_gu", [P, E, 2 * INTER])
        w_d = sb("w_d", [INTER, E, D])
        sg_t = sb("sg_t", [D, P])
        su_t = sb("su_t", [D, P])
        sd_t = sb("sd_t", [P, D])
        x_all = sb("x_all", [P, B * TOK])
        xb = sb("xb", [P, B * TPB, D])
        ident = sb("ident", [P, P])
        before = sb("before", [P, P])
        before_h = sb("before_h", [P, P], BF16)
        ones_h = sb("ones_h", [P, P], BF16)
        head_mask = sb("head_mask", [P, NH])
        iota_e = sb("iota_e", [P, E])
        zeros = sb("zeros", [P, E])
        wq_s = sb("wq_s", [D, D])
        wk_s = sb("wk_s", [DC, D])
        wv_s = sb("wv_s", [DC, D])
        wo_s = sb("wo_s", [D, D])
        bq_s = sb("bq_s", [D, 1])
        bqs_s = sb("bqs_s", [D, 1])
        bk_s = sb("bk_s", [D, 1])
        bv_s = sb("bv_s", [D, 1])
        bv_rep = sb("bv_rep", [D, P])
        bo_s = sb("bo_s", [P, D])
        bias_s = sb("bias_s", [P, D])
        gw_t = sb("gw_t", [D, E])
        gw_raw = sb("gw_raw", [E, D])
        gb_s = sb("gb_s", [P, E])
        eps_s = sb("eps_s", [P, TPB])
        minus_half = sb("minus_half", [P, TPB])
        empty = sb("empty", [P, FILL, PC])
        ctx_s = sb("ctx_s", [P, DC])
        raw_w = sb("raw_w", [P, 6, P])
        st1 = sb("st1", [P, TPB, 6])
        mv1 = sb("mv1", [P, TPB, 2])
        ve1 = sb("ve1", [P, TPB])
        rstd1 = sb("rstd1", [P, TPB])
        st2 = sb("st2", [P, TPB, 6])
        mv2 = sb("mv2", [P, TPB, 2])
        ve2 = sb("ve2", [P, TPB])
        rstd2 = sb("rstd2", [P, TPB])
        xn = sb("xn", [P, TPB, D])
        xn_t = sb("xn_t", [P, TOK])
        ctx_t = sb("ctx_t", [DC, P])
        q_t = sb("q_t", [P, TOK])
        k_t = sb("k_t", [P, KV])
        k_exp = sb("k_exp", [P, NH, KV])
        v_blk = sb("v_blk", [P, HP, VW])
        mx = sb("mx", [P, TPB, NH])
        p_s = sb("p_s", [P, TPB, NH * KV])
        p_t = sb("p_t", [P, TPB, HP * P])
        rsum = sb("rsum", [P, TPB * NH])
        o_s = sb("o_s", [P, TPB * NH, DH])
        o_t = sb("o_t", [P, TOK])
        xn2 = sb("xn2", [P, TPB, D])
        x2_t = sb("x2_t", [P, TOK])
        sig = sb("sig", [P, TPB, E])
        score = sb("score", [P, TPB, E])
        grp = sb("grp", [P, TPB, G + 4])
        grp_top = sb("grp_top", [P, TPB, 8])
        grp_rep = sb("grp_rep", [P, TPB, G + 4])
        msk = sb("msk", [P, TPB, E + 2])
        msk_rep = sb("msk_rep", [P, TPB, E + 2])
        top = sb("top", [P, TPB, 8])
        top_at = sb("top_at", [P, TPB, 8], U32)
        wsum = sb("wsum", [P, TPB])
        weight = sb("weight", [P, TPB, TOPK])
        chosen = sb("chosen", [P, TPB, E], BF16)
        ranks = sb("ranks", [P, 2, TPB, E])
        fill = sb("fill", [P, E])
        base2 = sb("base2", [P, E])
        next_page = [sb(f"next_page{t}", [P, E]) for t in range(TPB)]
        rank = sb("rank", [P, E])
        filled_to = sb("filled_to", [P, E])
        opens = sb("opens", [P, E])
        jump = sb("jump", [P, E])
        jumped = sb("jumped", [P, E])
        row = sb("row", [P, E])
        move = sb("move", [P, E])
        picked = sb("picked", [P, TOPK, E])
        expert_f = [sb(f"expert_f{t}", [P, TOPK]) for t in range(TPB)]
        place = [sb(f"place{t}", [P, TOPK]) for t in range(TPB)]
        place_i = [sb(f"place_i{t}", [P, TOPK], I32) for t in range(TPB)]
        payload = [sb(f"payload{t}", [P, TOPK, PC]) for t in range(TPB)]
        pg = [sb(f"pg{j}", [P, QUAD, PC]) for j in range(SLOTS)]
        codes = [sb(f"codes{j}", [P, QUAD], I32) for j in range(SLOTS)]
        scales = [sb(f"scales{j}", [P, QUAD]) for j in range(SLOTS)]
        digit = sb("digit", [1, QUAD])
        digits = sb("digits", [1, QUAD])
        expert_i = [sb(f"expert_i{j}", [1, 1], I32) for j in range(SLOTS)]
        spare = sb("spare", [P, 1])
        y_s = [sb(f"y_s{j}", [P, QUAD, D]) for j in range(SLOTS)]
        pxt = [sb(f"pxt{j}", [P, QUAD * P]) for j in range(2)]
        s_act = sb("s_act", [P, QUAD, INTER])
        h_s = [sb(f"h_s{j}", [P, QUAD, INTER]) for j in range(2)]
        h_t = [sb(f"h_t{j}", [INTER, QUAD, P]) for j in range(2)]
        sh_act = sb("sh_act", [P, TOK])
        sh_h = sb("sh_h", [P, TOK])
        routed = sb("routed", [P, TPB, D])
        w_flat = w_gu[:, :, :].rearrange("p e i -> p (e i)")
        ys = [w_flat[:, j * 2 * TOPK * D:(j + 1) * 2 * TOPK * D].rearrange("p (t k h) -> p t k h", t=2, k=TOPK)
              for j in range(SLOTS)]

        x_first, x_rest, const_in, gate_in = sem("x_first"), sem("x_rest"), sem("const_in"), sem("gate_in")
        ctx_in, raw_in, prefilled = sem("ctx_in"), sem("raw_in"), sem("prefilled")
        zeroed, made, halved, empty_ready = sem("zeroed"), sem("made"), sem("halved"), sem("empty_ready")
        dve_made, bvrep_ready, bias_done, bias_ready = sem("dve_made"), sem("bvrep_ready"), sem("bias_done"), sem("bias_ready")
        gwt_done, gwt_ready = sem("gwt_done"), sem("gwt_ready")
        st1_done, mv1_done, ve1_done, rstd1_done = sem("st1_done"), sem("mv1_done"), sem("ve1_done"), sem("rstd1_done")
        st2_done, mv2_done, ve2_done, rstd2_done = sem("st2_done"), sem("mv2_done"), sem("ve2_done"), sem("rstd2_done")
        xn_ready, xb_ready, xt_done, xts_ready = sem("xn_ready"), sem("xb_ready"), sem("xt_done"), sem("xts_ready")
        qkv_done, k_ready, q_ready = sem("qkv_done"), sem("k_ready"), sem("q_ready")
        kexp_ready, vblk_ready = sem("kexp_ready"), sem("vblk_ready")
        scores_done, mx_done, shifted, p_ready = sem("scores_done"), sem("mx_done"), sem("shifted"), sem("p_ready")
        pt_done, pt_ready, pv_done = sem("pt_done"), sem("pt_ready"), sem("pv_done")
        rsum_done, o_ready, ot_done, ot_ready = sem("rsum_done"), sem("o_ready"), sem("ot_done"), sem("ot_ready")
        wo_done, x2_done = sem("wo_done"), sem("x2_done")
        xn2_ready, x2t_done, x2t_ready = sem("xn2_ready"), sem("x2t_done"), sem("x2t_ready")
        logit_done, sig_ready, route, chosen_ready = sem("logit_done"), sem("sig_ready"), sem("route"), sem("chosen_ready")
        ranks_done, ranks_ready, placed = sem("ranks_done"), sem("ranks_ready"), sem("placed")
        payload_x, code_ready, spared, digits_done, packed = sem("payload_x"), sem("code_ready"), sem("spared"), sem("digits_done"), sem("packed")
        scattered = [sem(f"scattered{t}") for t in range(TPB)]
        wgu_done, wgu_ready, wd_done, wd_ready = sem("wgu_done"), sem("wgu_ready"), sem("wd_done"), sem("wd_ready")
        page_in = [sem(f"page_in{j}") for j in range(SLOTS)]
        y_out = [sem(f"y_out{j}") for j in range(SLOTS)]
        pxt_done, pxt_ready, gu_done, act_ready, h_ready = sem("pxt_done"), sem("pxt_ready"), sem("gu_done"), sem("act_ready"), sem("h_ready")
        ht_done, ht_ready, y_done, y_ready = sem("ht_done"), sem("ht_ready"), sem("y_done"), sem("y_ready")
        sh_gate, sh_silu, sh_up, sh_ready, sh_done, sh_added = (sem("sh_gate"), sem("sh_silu"), sem("sh_up"), sem("sh_ready"),
                                                                sem("sh_done"), sem("sh_added"))
        ys_in = [sem(f"ys_in{j}") for j in range(SLOTS)]
        empty_zeroed, added, summed, out_done = sem("empty_zeroed"), sem("added"), sem("summed"), sem("out_done")

        x_v = x.rearrange("b (t p) h -> p (b t) h", p=P)
        out_v = out.rearrange("b (t p) h -> p (b t) h", p=P)
        eg_v = eg.rearrange("(w j a) i h -> w (a i) j h", j=2, a=2)
        eu_v = eu.rearrange("(w j a) i h -> w (a i) j h", j=2, a=2)
        ed_v = ed.rearrange("(w e) h i -> w h e i", e=4)
        fill_v = pages[FIRST_FILL * P:PAGES * P, :].rearrange("(k p r) c -> k p (r c)", p=P, r=FILL)
        quad_v = pages.rearrange("(q g p) c -> q p g c", g=QUAD, p=P)
        ys_v = results.rearrange("(t p k) h -> p t k h", p=P, k=TOPK)

        def line(ap):
            return ap.rearrange("(a n) -> a n", a=1)

        def col(ap):
            return ap.rearrange("(p a) -> p a", a=1)

        def stages(b):
            if not isinstance(b, int):
                return True, True, True, True, True
            return b + 2 < B, b + 1 < B, 0 <= b < B, 1 <= b <= B, 2 <= b

        def phase1(body):
            for b in range(-1, 3):
                body(b)
            return range(3, B - 3), range(B - 3, B + 2)

        block = ctx.enter_context(nc.Block())

        @block.sync
        def _(sp):
            def load_ctx(b):
                for half in range(2):
                    sp.dma_start(ctx_s[half * KV:(half + 1) * KV, :], ctx_rows[bass.ds(b, 1), :, :].rearrange(
                        "a s d -> (a s) d")).then_inc(ctx_in, 16)

            def load_raw(w):
                sp.dma_start(raw_w[:, 0:2, :], eg_v[bass.ds(w, 1), :, :, :].rearrange(
                    "a p j h -> (a p) j h")).then_inc(raw_in, 16)
                sp.dma_start(raw_w[:, 2:4, :], eu_v[bass.ds(w, 1), :, :, :].rearrange(
                    "a p j h -> (a p) j h")).then_inc(raw_in, 16)
                sp.dma_start(raw_w[:, 4:6, :].rearrange("p j (e i) -> p (j e) i", e=2), ed_v[
                    bass.ds(w, 1), :, :, :].rearrange("a h e i -> (a h) e i")).then_inc(raw_in, 16)

            def prefill(k):
                sp.wait_ge(prefilled, 16 * (k + 1))
                sp.dma_start(fill_v[bass.ds(k, 1), :, :].rearrange("k p c -> (k p) c"),
                             empty[:, :, :].rearrange("p r c -> p (r c)")).then_inc(prefilled, 16)

            def load_batch(b):
                sp.wait_ge(xt_done, b + 1)
                load_ctx(b + 1)
                sp.wait_ge(wd_done, b + 1)
                load_raw(b)

            sp.dma_start(xb[:, 0:TPB, :], x_v[:, 0:TPB, :]).then_inc(x_first, 16)
            load_ctx(0)
            for dst, src in ((wq_s, wq), (wk_s, wk), (wv_s, wv), (bq_s, col(bq)), (bk_s, col(bk)), (bv_s, col(bv)), (wo_s, wo)):
                sp.dma_start(dst[:, :], src).then_inc(const_in, 16)
            for dst, src, n in ((bo_s, bo, D), (gb_s, gate_bias, E)):
                sp.dma_start(dst[:, :], line(src).to_broadcast([P, n])).then_inc(const_in, 16)
            sp.dma_start(gw_raw[:, :], gate_w).then_inc(gate_in, 16)
            sp.dma_start(xb[:, TPB:, :], x_v[:, TPB:, :]).then_inc(x_rest, 16)
            sp.dma_start(raw_w[:, 0, :], sg).then_inc(raw_in, 16)
            sp.dma_start(raw_w[:, 2, :], su).then_inc(raw_in, 16)
            sp.dma_start(raw_w[:, 4, :], sd).then_inc(raw_in, 16)
            sp.wait_ge(empty_ready, 1)
            sp.dma_start(pages[0:FIRST_FILL * P, :].rearrange("(p r) c -> p (r c)", p=P),
                         empty[:, 0:FIRST_FILL, :].rearrange("p r c -> p (r c)")).then_inc(prefilled, 16)
            for b in range(2):
                load_batch(b)
                for k in range(4):
                    prefill(4 * b + k)
            with sp.Fori(2, B - 1) as b:
                load_batch(b)
                prefill(b + 6)
            sp.wait_ge(wd_done, B)
            load_raw(B - 1)
            for t in range(TPB):
                sp.wait_ge(scattered[t], 16 * TOPK * B)

            def load_quads(i, first):
                for j in range(SLOTS):
                    q = i * SLOTS + j
                    if not first:
                        sp.wait_ge(code_ready, q - SLOTS + 1)
                    sp.dma_start(pg[j][:, :, :], quad_v[bass.ds(q, 1), :, :, :].rearrange(
                        "a p g c -> (a p) g c")).then_inc(page_in[j], 16)

            load_quads(0, True)
            with sp.Fori(1, NQ // SLOTS) as i:
                load_quads(i, False)

            for j in range(SLOTS):
                sp.wait_ge(y_out[j], 16 * QUAD * NQ // SLOTS)
            sp.wait_ge(gu_done, NQ)

            def load_results(i, first):
                for j in range(SLOTS):
                    n = i * SLOTS + j
                    if not first:
                        sp.wait_ge(summed, n - SLOTS + 1)
                    sp.dma_start(ys[j], ys_v[:, bass.ds(n * 2, 2), :, :]).then_inc(ys_in[j], 16)

            load_results(0, True)
            with sp.Fori(1, B // SLOTS) as i:
                load_results(i, False)
            sp.wait_ge(out_done, 16 * B)

        @block.gpsimd
        def _(pool):
            pool.memset(ident[:, :], 0.0).then_inc(zeroed, 1)
            pool.memset(v_blk[:, :, :], 0.0).then_inc(zeroed, 1)
            pool.memset(before[:, :], 1.0).then_inc(zeroed, 1)
            pool.memset(head_mask[:, :], 1.0).then_inc(zeroed, 1)
            pool.memset(zeros[:, :], 0.0).then_inc(made, 1)
            pool.memset(eps_s[:, :], EPS).then_inc(made, 1)
            pool.memset(minus_half[:, :], -0.5).then_inc(made, 1)
            pool.memset(grp[:, :, G:], BIG).then_inc(made, 1)
            pool.memset(msk[:, :, E:], BIG).then_inc(made, 1)
            pool.wait_ge(zeroed, 4)
            pool.affine_select(out=ident[:, :], in_=ident[:, :], compare_op=ALU.not_equal, fill=1.0, base=0,
                               pattern=[[-1, P]], channel_multiplier=1).then_inc(made, 1)
            pool.affine_select(out=before[:, :], in_=before[:, :], compare_op=ALU.is_ge, fill=0.0, base=-1,
                               pattern=[[1, P]], channel_multiplier=-1).then_inc(made, 1)
            pool.affine_select(out=head_mask[:, :], in_=head_mask[:, :], compare_op=ALU.is_ge, fill=0.0, base=0,
                               pattern=[[-DH, NH]], channel_multiplier=1).then_inc(halved, 1)
            pool.wait_ge(halved, 1)
            pool.affine_select(out=head_mask[:, :], in_=head_mask[:, :], compare_op=ALU.is_ge, fill=0.0, base=DH - 1,
                               pattern=[[DH, NH]], channel_multiplier=-1).then_inc(made, 1)
            pool.iota(iota_e[:, :], [[1, E]], base=0, channel_multiplier=0,
                      allow_small_or_imprecise_dtypes=True).then_inc(made, 1)
            pool.iota(base2[:, :], [[P, E]], base=2 * P, channel_multiplier=0,
                      allow_small_or_imprecise_dtypes=True).then_inc(made, 1)
            for t in range(TPB):
                pool.iota(payload[t][:, :, CODE].bitcast(I32), [[1, TOPK]], base=t * P * TOPK - TOK * TOPK,
                          channel_multiplier=TOPK).then_inc(made, 1)

            def rstd(n, mv_done, ve_done, rstd_done, mv, ve, r):
                pool.wait_ge(mv_done, TPB * (n + 1))
                pool.tensor_tensor(ve[:, :], mv[:, :, 1], eps_s[:, :], ALU.add).then_inc(ve_done, 1)
                pool.wait_ge(ve_done, n + 1)
                pool.tensor_tensor(r[:, :], ve[:, :], minus_half[:, :], ALU.pow).then_inc(rstd_done, 1)

            def add_biases(n):
                pool.wait_ge(xn_ready, TPB * (n + 1))
                xt = xb[:, bass.ds(TPB * n, TPB), :]
                pool.tensor_tensor(xt, xt, bias_s[:, :].unsqueeze(1).to_broadcast([P, TPB, D]), ALU.add).then_inc(xb_ready, 1)

            def expand_k(n):
                pool.wait_ge(k_ready, n + 1)
                pool.tensor_tensor(k_exp[:, :, :], k_t[:, :].unsqueeze(1).to_broadcast([P, NH, KV]),
                                   head_mask[:, :].unsqueeze(2).to_broadcast([P, NH, KV]),
                                   ALU.mult).then_inc(kexp_ready, 1)

            def wait_payload(n, t):
                if t == 0:
                    pool.wait_ge(spared, n)
                pool.wait_ge(placed, PLACE_STEPS * (TPB * n + t + 1))
                pool.wait_ge(payload_x, TPB * n + t + 1)
                pool.wait_ge(prefilled, 16 * (n + FILLS_AHEAD))

            def scatter(t):
                for k in range(TOPK):
                    pool.indirect_dma_start(out=pages[:, :], out_offset=bass.IndirectOffsetOnAxis(
                        ap=place_i[t][:, k:k + 1], axis=0), in_=payload[t][:, k, :], in_offset=None,
                        bounds_check=PAGES * P - 1, oob_is_err=False).then_inc(scattered[t], 16)

            def body(b):
                s0, s1, s2, s3, s4 = stages(b)
                if s0:
                    rstd(b + 2, mv1_done, ve1_done, rstd1_done, mv1, ve1, rstd1)
                if s3:
                    rstd(b - 1, mv2_done, ve2_done, rstd2_done, mv2, ve2, rstd2)
                if s1:
                    expand_k(b + 1)
                if s4:
                    wait_payload(b - 2, 0)
                    pool.tensor_tensor(spare[:, :], zeros[:, 0:1], zeros[:, 0:1], ALU.add).then_inc(spared, 1)
                    scatter(0)
                    wait_payload(b - 2, 1)
                if s1:
                    if isinstance(b, int) and b == -1:
                        pool.wait_ge(bias_ready, 1)
                    add_biases(b + 1)
                if s4:
                    scatter(1)

            rstd(0, mv1_done, ve1_done, rstd1_done, mv1, ve1, rstd1)
            loop, last = phase1(body)
            with pool.Fori(loop.start, loop.stop) as b:
                body(b)
            for b in last:
                body(b)

            def quads(i):
                for j in range(SLOTS):
                    q = i * SLOTS + j
                    pool.wait_ge(code_ready, q + 1)
                    pool.wait_ge(y_ready, q + 1)
                    pool.wait_ge(spared, q + B)
                    pool.tensor_tensor(spare[:, :], zeros[:, 0:1], zeros[:, 0:1], ALU.add).then_inc(spared, 1)
                    for g in range(QUAD):
                        pool.indirect_dma_start(out=results[:, :], out_offset=bass.IndirectOffsetOnAxis(
                            ap=codes[j][:, g:g + 1], axis=0), in_=y_s[j][:, g, :], in_offset=None,
                            bounds_check=B * TOK * TOPK - 1, oob_is_err=False).then_inc(y_out[j], 16)

            with pool.Fori(0, NQ // SLOTS) as i:
                quads(i)

        @block.scalar
        def _(act):
            def copy(dst, src):
                return act.activation(dst, src, ACT.Copy)

            def transposed_x(n):
                act.wait_ge(xt_done, n + 1)
                copy(xn_t[:, :], bank_q[:, 0:TOK]).then_inc(xts_ready, 1)
                copy(ctx_t[:, :], bank_q[0:DC, TOK:TOK + P]).then_inc(xts_ready, 1)

            def evacuate_qk(n):
                act.wait_ge(qkv_done, n + 1)
                act.activation(k_t[:, :], bank_q[:, TOK:TOK + KV], ACT.Identity, bias=bk_s[:, 0:1]).then_inc(k_ready, 1)
                act.activation(q_t[:, :], bank_q[:, 0:TOK], ACT.Identity, bias=bqs_s[:, 0:1], scale=SCALE).then_inc(q_ready, 1)

            def transposed_x2(n):
                act.wait_ge(x2t_done, n + 1)
                copy(x2_t[:, :], bank_r[:, 0:TOK]).then_inc(x2t_ready, 1)
                copy(x_all[:, bass.ds(n * TOK, TOK)], bank_r[:, 0:TOK]).then_inc(x2t_ready, 1)

            def exps(b, j):
                act.wait_ge(shifted, TPB * b + j + 1)
                act.activation(p_s[:, j, :], p_s[:, j, :], ACT.Exp).then_inc(p_ready, 1)

            def copy_pt(b, j):
                act.wait_ge(pt_done, TPB * b + j + 1)
                copy(p_t[:, j, :], bank_s[j][:, :]).then_inc(pt_ready, 1)

            def sigmoid_exp(n):
                act.wait_ge(logit_done, n + 1)
                act.activation(sig[:, :, :].rearrange("p t e -> p (t e)"), bank_r[:, TOK:TOK + TPB * E], ACT.Exp,
                               scale=-1.0).then_inc(sig_ready, 1)

            def copy_ranks(n):
                act.wait_ge(ranks_done, n + 1)
                act.wait_ge(placed, PLACE_STEPS * TPB * n)
                copy(ranks[:, :, :, :].rearrange("p a t e -> p (a t e)"), bank_r[:, 0:TOK]).then_inc(ranks_ready, 1)

            def fill_payload(n, t):
                act.wait_ge(xn2_ready, TPB * n + t + 1)
                act.wait_ge(scattered[t], 16 * TOPK * n)
                copy(payload[t][:, :, 0:D], xn2[:, t, :].unsqueeze(1).to_broadcast([P, TOPK, D])).then_inc(payload_x, 1)

            def gate_up_weights(w):
                act.wait_ge(wgu_done, w + 2)
                copy(w_gu[:, bass.ds(4 * w, 4), :].rearrange("p e (u i) -> p u e i", u=2),
                     bank_w[:, :].rearrange("p (u e i) -> p u e i", u=2, e=4)).then_inc(wgu_ready, 1)

            def down_weights(w):
                act.wait_ge(wd_done, w + 2)
                for a in range(2):
                    copy(w_d[:, bass.ds(4 * w, 4), :].rearrange("p (j a) h -> p j a h", a=2)[:, :, a, :],
                         bank_w[a * INTER:(a + 1) * INTER, 0:2 * P].rearrange("p (j h) -> p j h", j=2)).then_inc(wd_ready, 1)

            def body(b):
                s0, s1, s2, s3, s4 = stages(b)
                if s4:
                    fill_payload(b - 2, 0)
                if s2:
                    exps(b, 0)
                if s1:
                    transposed_x(b + 1)
                if s4:
                    fill_payload(b - 2, 1)
                if s2:
                    exps(b, 1)
                    copy_pt(b, 0)
                if s1:
                    evacuate_qk(b + 1)
                if s3:
                    transposed_x2(b - 1)
                if s2:
                    copy_pt(b, 1)
                if s3:
                    sigmoid_exp(b - 1)
                if s2:
                    gate_up_weights(b)
                if s2:
                    down_weights(b)
                if s2:
                    act.wait_ge(ot_done, b + 1)
                    copy(o_t[:, :], bank_o[:, 0:TOK]).then_inc(ot_ready, 1)
                if s3:
                    copy_ranks(b - 1)

            act.wait_ge(gwt_done, 1)
            copy(gw_t[:, :], bank_r[:, 0:E]).then_inc(gwt_ready, 1)
            act.wait_ge(dve_made, 4)
            act.wait_ge(const_in, 16 * NCONST)
            act.wait_ge(wgu_done, 1)
            copy(sg_t[:, :], bank_w[:, 0:P]).then_inc(wgu_ready, 1)
            copy(su_t[:, :], bank_w[:, P:2 * P]).then_inc(wgu_ready, 1)
            act.wait_ge(wd_done, 1)
            copy(sd_t[:, :], bank_w[:, 0:P]).then_inc(wd_ready, 2)
            loop, last = phase1(body)
            with act.Fori(loop.start, loop.stop) as b:
                body(b)
            for b in last:
                body(b)

            def page_x(q, j):
                act.wait_ge(pxt_done, q + 1)
                copy(pxt[j % 2][:, :], xt_ps[j % 2]).then_inc(pxt_ready, 1)

            def page_result(i, j, first):
                act.wait_ge(y_done, i * SLOTS + j + 1)
                if not first:
                    act.wait_ge(y_out[j], 16 * QUAD * i)
                act.wait_ge(code_ready, i * SLOTS + j + 1)
                for g in range(QUAD):
                    scaled = act.activation(y_s[j][:, g, :], bank_o[:, g * D:(g + 1) * D], ACT.Identity,
                                            scale=scales[j][:, g:g + 1])
                scaled.then_inc(y_ready, 1)

            def quads(i, first, last):
                for j in range(SLOTS):
                    q = i * SLOTS + j
                    act.wait_ge(gu_done, q + 1)
                    if not (first and j == 0):
                        act.wait_ge(h_ready, q)
                    act.activation(s_act[:, :, :], gu_ps[j % 2].rearrange("p (g u i) -> p g u i", g=QUAD, u=2)[:, :, 0, :],
                                   ACT.Silu).then_inc(act_ready, 1)
                    if j == 0:
                        act.wait_ge(sh_gate, i + 1)
                        act.activation(sh_act[:, :], bank_r[:, 0:TOK], ACT.Silu).then_inc(sh_silu, 1)
                    if j + 1 < SLOTS:
                        page_x(q + 1, j + 1)
                    elif not last:
                        page_x(q + 1, 0)
                    if j > 0:
                        page_result(i, j - 1, first)
                page_result(i, SLOTS - 1, first)

            page_x(0, 0)
            quads(0, True, False)
            with act.Fori(1, NQ // SLOTS - 1) as i:
                quads(i, False, False)
            quads(NQ // SLOTS - 1, False, True)

            def store(n):
                act.wait_ge(summed, n + 1)
                act.dma_start(out_v[:, bass.ds(n * TPB, TPB), :], xb[:, bass.ds(n * TPB, TPB), :]).then_inc(out_done, 16)

            with act.Fori(0, B) as n:
                store(n)

        @block.vector
        def _(dve):
            dve.memset(empty[:, :, :], 0.0).then_inc(empty_zeroed, 1)
            dve.wait_ge(empty_zeroed, 1)
            dve.memset(empty[:, :, CODE:CODE + 1].bitcast(I32), NO_CODE).then_inc(empty_ready, 1)
            dve.wait_ge(made, MADE)
            dve.memset(v_blk[0:KV, :, DH:DH + 1], 1.0).then_inc(dve_made, 1)
            dve.memset(v_blk[KV:P, :, VW - 1:VW], 1.0).then_inc(dve_made, 1)
            dve.memset(fill[:, :], 0.0)
            dve.memset(ones_h[:, :], 1.0)
            for g in range(QUAD):
                dve.memset(digit[:, g:g + 1], float(E ** g))
            dve.memset(next_page[1][:, :], float(E)).then_inc(dve_made, 1)

            def x_tile(i):
                return xb[:, bass.ds(i, 1), :].rearrange("p t h -> p (t h)")

            def stats(n, t, st, st_done):
                dve.bn_stats(st[:, t, :], x_tile(TPB * n + t)).then_inc(st_done, 1)

            def aggregate(st, mv, mv_done):
                for t in range(TPB):
                    dve.bn_aggr(mv[:, t, :], st[:, t, :]).then_inc(mv_done, 1)

            def normalize(n, dst, mv, r, r_done, ready):
                dve.wait_ge(r_done, n + 1)
                for t in range(TPB):
                    dve.tensor_scalar(dst[:, t, :], x_tile(TPB * n + t), mv[:, t, 0:1], r[:, t:t + 1],
                                      ALU.subtract, ALU.mult).then_inc(ready, 1)


            def maxima(b, j):
                dve.wait_ge(scores_done, TPB * b + j + 1)
                dve.tensor_reduce(mx[:, j, :], bank_s[j][:, :].rearrange("p (h k) -> p h k", k=KV), AX.X,
                                  ALU.max).then_inc(mx_done, 1)

            def shift(b, j):
                dve.wait_ge(mx_done, TPB * b + j + 1)
                dve.tensor_tensor(p_s[:, j, :].rearrange("p (h k) -> p h k", k=KV),
                                  bank_s[j][:, :].rearrange("p (h k) -> p h k", k=KV),
                                  mx[:, j, :].unsqueeze(2).to_broadcast([P, NH, KV]), ALU.subtract).then_inc(shifted, 1)

            def routing(n, between):
                at = [0]

                def chained(ins):
                    at[0] += 1
                    ins.then_inc(route, 1)

                def settle():
                    dve.wait_ge(route, n * ROUTE_STEPS + at[0])

                def settle_between():
                    settle()
                    if between:
                        between.pop(0)()

                flat = lambda t: t[:, :, :].rearrange("p t e -> p (t e)")
                dve.wait_ge(sig_ready, n + 1)
                chained(dve.tensor_scalar(flat(sig), flat(sig), 1.0, None, ALU.add))
                settle()
                chained(dve.reciprocal(flat(score), flat(sig)))
                settle()
                chained(dve.tensor_tensor(score[:, :, :], score[:, :, :], gb_s[:, :].unsqueeze(1).to_broadcast([P, TPB, E]), ALU.add))
                settle()
                chained(dve.tensor_reduce(grp[:, :, 0:G], score[:, :, :].rearrange("p t (g e) -> p t g e", g=G), AX.X, ALU.max))
                settle_between()
                for t in range(TPB):
                    chained(dve.max(grp_top[:, t, :], grp[:, t, :]))
                settle_between()
                for t in range(TPB):
                    chained(dve.match_replace(grp_rep[:, t, :], grp_top[:, t, :], grp[:, t, :], -BIG))
                settle()
                for t in range(TPB):
                    chained(dve.scalar_tensor_tensor(
                        out=msk[:, t, 0:E].rearrange("p (g e) -> p g e", g=G),
                        in0=grp_rep[:, t, 0:G].unsqueeze(2).to_broadcast([P, G, E // G]), scalar=TAKEN,
                        in1=score[:, t, :].rearrange("p (g e) -> p g e", g=G), op0=ALU.is_lt, op1=ALU.mult))
                settle_between()
                for t in range(TPB):
                    chained(dve.max(top[:, t, :], msk[:, t, :]))
                settle_between()
                for t in range(TPB):
                    chained(dve.match_replace(msk_rep[:, t, :], top[:, t, :], msk[:, t, :], -BIG))
                    chained(dve.max_index(top_at[:, t, :], top[:, t, :], msk[:, t, :]))
                chained(dve.tensor_reduce(wsum[:, :], top[:, :, 8 - TOPK:8], AX.X, ALU.add))
                settle()
                dve.tensor_scalar(chosen[:, :, :], msk_rep[:, :, 0:E], TAKEN, None, ALU.is_lt).then_inc(chosen_ready, 1)
                chained(dve.tensor_scalar(wsum[:, :], wsum[:, :], 1e-8, None, ALU.add))
                settle()
                chained(dve.reciprocal(wsum[:, :], wsum[:, :]))
                settle()
                chained(dve.tensor_tensor(weight[:, :, :], top[:, :, 8 - TOPK:8],
                                          wsum[:, :].unsqueeze(2).to_broadcast([P, TPB, TOPK]), ALU.mult))
                assert at[0] == ROUTE_STEPS

            def place_steps(n, t):
                at = [0]

                def chained(ins):
                    at[0] += 1
                    ins.then_inc(placed, 1)

                def settle():
                    dve.wait_ge(placed, PLACE_STEPS * (TPB * n + t) + at[0])

                def ranks_in_page():
                    dve.wait_ge(ranks_ready, n + 1)
                    settle()
                    chained(dve.tensor_tensor(rank[:, :], ranks[:, 0, t, :], fill[:, :], ALU.add))
                    chained(dve.tensor_tensor(filled_to[:, :], ranks[:, 1, t, :], fill[:, :], ALU.add))

                def open_pages():
                    settle()
                    dve.wait_ge(scattered[t], 16 * TOPK * n)
                    chained(dve.tensor_scalar(opens[:, :], filled_to[:, :], float(P), None, ALU.is_gt))
                    chained(dve.tensor_copy(payload[t][:, :, EXPERT].bitcast(U32), top_at[:, t, 8 - TOPK:8]))
                    chained(dve.tensor_copy(expert_f[t][:, :], top_at[:, t, 8 - TOPK:8]))
                    chained(dve.tensor_copy(payload[t][:, :, WEIGHT], weight[:, t, :]))
                    code = payload[t][:, :, CODE].bitcast(I32)
                    chained(dve.tensor_scalar(code, code, TOK * TOPK, None, ALU.add))

                def number_pages():
                    settle()
                    chained(dve.tensor_tensor_scan(next_page[t][:, :], opens[:, :], zeros[:, :], next_page[1 - t][:, E - 1:E],
                                                   ALU.add, ALU.add))
                    chained(dve.scalar_tensor_tensor(out=fill[:, :], in0=opens[:, :], scalar=-float(P), in1=filled_to[:, :],
                                                     op0=ALU.mult, op1=ALU.add))
                    chained(dve.scalar_tensor_tensor(out=row[:, :], in0=rank[:, :], scalar=-2.0 * P, in1=base2[:, :],
                                                     op0=ALU.add, op1=ALU.add))

                def jumps():
                    settle()
                    chained(dve.scalar_tensor_tensor(out=jump[:, :], in0=next_page[t][:, :], scalar=float(P), in1=base2[:, :],
                                                     op0=ALU.mult, op1=ALU.subtract))

                def apply_jumps():
                    settle()
                    chained(dve.scalar_tensor_tensor(out=jumped[:, :], in0=rank[:, :], scalar=float(P), in1=jump[:, :],
                                                     op0=ALU.is_ge, op1=ALU.mult))
                    chained(dve.scalar_tensor_tensor(out=move[:, :], in0=jump[:, :], scalar=float(P), in1=opens[:, :],
                                                     op0=ALU.add, op1=ALU.mult))

                def rows():
                    settle()
                    chained(dve.tensor_tensor(row[:, :], row[:, :], jumped[:, :], ALU.add))
                    chained(dve.tensor_tensor(base2[:, :], base2[:, :], move[:, :], ALU.add))

                def pick():
                    settle()
                    for k in range(TOPK):
                        chained(dve.scalar_tensor_tensor(out=picked[:, k, :], in0=iota_e[:, :],
                                                             scalar=expert_f[t][:, k:k + 1], in1=row[:, :],
                                                             op0=ALU.is_equal, op1=ALU.mult, accum_out=place[t][:, k:k + 1]))

                def to_int():
                    settle()
                    chained(dve.tensor_copy(place_i[t][:, :], place[t][:, :]))
                    assert at[0] == PLACE_STEPS

                return [ranks_in_page, open_pages, number_pages, jumps, apply_jumps, rows, pick, to_int]

            def v_blocks(n):
                dve.wait_ge(q_ready, n + 1)
                dve.wait_ge(pv_done, n)
                for h in range(2):
                    rows = slice(h * KV, (h + 1) * KV)
                    dve.tensor_copy(v_blk[rows, :, h * (DH + 1):h * (DH + 1) + DH],
                                    bank_q[rows, TOK + KV:TOK + KV + D].rearrange("p (a h d) -> p a h d", h=2, d=DH)[
                                        :, :, h, :]).then_inc(vblk_ready, 1)

            def divide_by_sum(b):
                pv = bank_o[:, 0:TPB * HP * VW].rearrange("p (h e) -> p h e", e=DH + 1)
                dve.wait_ge(pv_done, b + 1)
                dve.reciprocal(rsum[:, :], pv[:, :, DH]).then_inc(rsum_done, 1)
                dve.wait_ge(rsum_done, b + 1)
                dve.tensor_tensor(o_s[:, :, :], pv[:, :, 0:DH], rsum[:, :].unsqueeze(2).to_broadcast([P, TPB * NH, DH]),
                                  ALU.mult).then_inc(o_ready, 1)

            def body(b):
                s0, s1, s2, s3, s4 = stages(b)
                if s1:
                    dve.wait_ge(xt_done, b + 1)
                    normalize(b + 1, xn, mv1, rstd1, rstd1_done, xn_ready)
                if s3:
                    dve.wait_ge(x2_done, b)
                    for t in range(TPB):
                        stats(b - 1, t, st2, st2_done)
                if s0:
                    dve.wait_ge(st1_done, TPB * (b + 3))
                    dve.wait_ge(xn_ready, TPB * (b + 2))
                if s3:
                    dve.wait_ge(st2_done, TPB * b)
                if s2:
                    maxima(b, 0)
                if s3:
                    aggregate(st2, mv2, mv2_done)
                if s0:
                    aggregate(st1, mv1, mv1_done)
                if s2:
                    shift(b, 0)
                    maxima(b, 1)
                    shift(b, 1)
                if s3:
                    dve.wait_ge(payload_x, TPB * (b - 1))
                    dve.wait_ge(x2t_done, b - 1)
                    normalize(b - 1, xn2, mv2, rstd2, rstd2_done, xn2_ready)
                if s4:
                    for step in place_steps(b - 2, 0):
                        step()
                    for step in place_steps(b - 2, 1):
                        step()
                between = []
                if not isinstance(b, int) or b + 3 < B:
                    def first_stats():
                        dve.wait_ge(mv1_done, TPB * (b + 3))
                        stats(b + 3, 0, st1, st1_done)
                    between += [first_stats, lambda: stats(b + 3, 1, st1, st1_done)]
                if s2:
                    between += [lambda: divide_by_sum(b)]
                if s1:
                    between += [lambda: v_blocks(b + 1)]
                if s3:
                    routing(b - 1, between)
                for step in between:
                    step()
                if s2:
                    dve.wait_ge(wo_done, b + 1)
                    dve.wait_ge(xb_ready, b + 1)
                    xt = xb[:, bass.ds(TPB * b, TPB), :]
                    dve.tensor_tensor(xt, bank_o[:, TOK:2 * TOK].rearrange("p (t h) -> p t h", h=D), xt,
                                      ALU.add).then_inc(x2_done, 1)
            dve.wait_ge(x_first, 16)
            for t in range(TPB):
                stats(0, t, st1, st1_done)
            dve.wait_ge(st1_done, TPB)
            aggregate(st1, mv1, mv1_done)
            dve.tensor_copy(before_h[:, :], before[:, :])
            dve.wait_ge(const_in, 16 * NCONST)
            dve.tensor_scalar(bqs_s[:, :], bq_s[:, :], SCALE, None, ALU.mult).then_inc(dve_made, 1)
            dve.tensor_scalar(bv_rep[:, :], wo_s[:, :], 0.0, bv_s[:, 0:1], ALU.mult, ALU.add).then_inc(bvrep_ready, 1)
            dve.wait_ge(bias_done, 1)
            dve.tensor_tensor(bias_s[:, :], bank_o[:, 0:D], bo_s[:, :], ALU.add).then_inc(bias_ready, 1)
            dve.wait_ge(x_rest, 16)
            dve.wait_ge(mv1_done, TPB)
            for t in range(TPB):
                stats(1, t, st1, st1_done)
            loop, last = phase1(body)
            with dve.Fori(loop.start, loop.stop) as b:
                body(b)
            for b in last:
                body(b)

            def pack_experts(i, j, n):
                dve.wait_ge(page_in[j], 16 * (i + 1))
                if not (isinstance(n, int) and n == 0):
                    dve.wait_ge(packed, n)
                dve.tensor_tensor(digits[:, :], pg[j][0:1, :, EXPERT].bitcast(I32), digit[:, :], ALU.mult).then_inc(digits_done, 1)
                dve.wait_ge(digits_done, n + 1)
                with nc.allow_low_precision(reason="whole numbers below 2 ** 24 are exact in float32"):
                    dve.tensor_reduce(expert_i[j][:, :], digits[:, :], AX.X, ALU.add).then_inc(packed, 1)

            def quads(i, first, last):
                for j in range(SLOTS):
                    q = i * SLOTS + j
                    dve.wait_ge(act_ready, q + 1)
                    dve.tensor_tensor(h_s[j % 2][:, :, :], gu_ps[j % 2].rearrange("p (g u i) -> p g u i", g=QUAD, u=2)[:, :, 1, :],
                                      s_act[:, :, :], ALU.mult).then_inc(h_ready, 1)
                    if not first:
                        dve.wait_ge(y_out[j], 16 * QUAD * i)
                    dve.tensor_copy(scales[j][:, :], pg[j][:, :, WEIGHT])
                    dve.tensor_copy(codes[j][:, :], pg[j][:, :, CODE].bitcast(I32)).then_inc(code_ready, 1)
                    if j + 1 < SLOTS:
                        pack_experts(i, j + 1, q + 1)
                    elif not last:
                        pack_experts(i + 1, 0, q + 1)
                    if j == 2:
                        dve.wait_ge(sh_silu, i + 1)
                        dve.wait_ge(sh_up, i + 1)
                        dve.tensor_tensor(sh_h[:, :], bank_r[:, TOK:2 * TOK], sh_act[:, :], ALU.mult).then_inc(sh_ready, 1)
                    dve.wait_ge(ht_done, q + 1)
                    for a in range(2):
                        copied = dve.tensor_copy(h_t[j % 2][:, :, :].rearrange("p (g a) t -> p g a t", a=2)[:, :, a, :],
                                               bank_q[a * INTER:(a + 1) * INTER, 0:QUAD // 2 * P].rearrange(
                                                   "p (g t) -> p g t", t=P))
                    copied.then_inc(ht_ready, 1)
                dve.wait_ge(sh_done, i + 1)
                xt = xb[:, bass.ds(TPB * i, TPB), :]
                dve.tensor_tensor(xt, bank_w[:, 0:TOK].rearrange("p (t h) -> p t h", h=D), xt, ALU.add).then_inc(sh_added, 1)

            pack_experts(0, 0, 0)
            quads(0, True, False)
            with dve.Fori(1, NQ // SLOTS - 1) as i:
                quads(i, False, False)
            quads(NQ // SLOTS - 1, False, True)
            dve.wait_ge(sh_added, B)

            def combine(i, first):
                for j in range(SLOTS):
                    n = i * SLOTS + j
                    dve.wait_ge(ys_in[j], 16 * (i + 1))
                    if not (first and j == 0):
                        dve.wait_ge(summed, n)
                    dve.tensor_reduce(routed[:, :, :], ys[j].rearrange("p t k h -> p t h k"), AX.X, ALU.add).then_inc(added, 1)
                    dve.wait_ge(added, n + 1)
                    xt = xb[:, bass.ds(TPB * n, TPB), :]
                    dve.tensor_tensor(xt, routed[:, :, :], xt, ALU.add).then_inc(summed, 1)

            combine(0, True)
            with dve.Fori(1, B // SLOTS) as i:
                combine(i, False)


        @block.tensor
        def _(pe):
            def transposes(outs, ins, done):
                for o, i in zip(outs, ins):
                    k = i.shape[0]
                    last = pe.transpose(o, i, ident[0:k, 0:k])
                last.then_inc(done, 1)

            def mm(dst, w, v):
                return pe.matmul(dst, w, v, start=True, stop=True)

            def transpose_x(n):
                pe.wait_ge(xn_ready, TPB * (n + 1))
                pe.wait_ge(ctx_in, 32 * (n + 1))
                pe.wait_ge(q_ready, n)
                pe.wait_ge(vblk_ready, 2 * n)
                transposes([bank_q[:, t * P:(t + 1) * P] for t in range(TPB)] + [bank_q[0:DC, TOK:TOK + P]],
                           [xn[:, t, :] for t in range(TPB)] + [ctx_s[:, :]], xt_done)

            def project(n):
                pe.wait_ge(xts_ready, 2 * (n + 1))
                mm(bank_q[:, 0:TOK], wq_s[:, :], xn_t[:, :])
                mm(bank_q[:, TOK:TOK + KV], wk_s[:, :], ctx_t[:, 0:KV])
                mm(bank_q[:, TOK + KV:TOK + KV + D], ctx_t[:, :], wv_s[:, :]).then_inc(qkv_done, 1)

            def transpose_x2(n):
                pe.wait_ge(xn2_ready, TPB * (n + 1))
                pe.wait_ge(ranks_ready, n)
                transposes([bank_r[:, t * P:(t + 1) * P] for t in range(TPB)], [xn2[:, t, :] for t in range(TPB)], x2t_done)

            def logits(n):
                pe.wait_ge(x2t_ready, 2 * (n + 1))
                for t in range(TPB):
                    last = mm(bank_r[:, TOK + t * E:TOK + (t + 1) * E], x2_t[:, t * P:(t + 1) * P], gw_t[:, :])
                last.then_inc(logit_done, 1)

            def count_choosers(n):
                pe.wait_ge(chosen_ready, n + 1)
                m = chosen[:, :, :].rearrange("p t e -> p (t e)")
                mm(bank_r[:, 0:TPB * E], before_h[:, :], m)
                mm(bank_r[:, TPB * E:2 * TPB * E], ones_h[:, :], m).then_inc(ranks_done, 1)

            def gate_up_weights(w, slots):
                pe.wait_ge(raw_in, 48 * (w + 1))
                pe.wait_ge(wd_ready, 2 * w)
                transposes([bank_w[:, i * P:(i + 1) * P] for i in range(len(slots))], [raw_w[:, s, :] for s in slots], wgu_done)

            def down_weights(w):
                pe.wait_ge(wgu_ready, w + 2)
                transposes([bank_w[:, i * P:(i + 1) * P] for i in range(2)], [raw_w[:, 4 + i, :] for i in range(2)], wd_done)

            def scores(b):
                pe.wait_ge(q_ready, b + 1)
                pe.wait_ge(kexp_ready, b + 1)
                for j in range(TPB):
                    pe.wait_ge(pt_ready, TPB * b)
                    for half in range(2):
                        last = mm(bank_s[j][:, half * 512:(half + 1) * 512], q_t[:, j * P:(j + 1) * P],
                                  k_exp[:, half * HP:(half + 1) * HP, :].rearrange("p h k -> p (h k)"))
                    last.then_inc(scores_done, 1)

            def transpose_p(b, j):
                pe.wait_ge(p_ready, TPB * b + j + 1)
                transposes([bank_s[j][:, a * P:(a + 1) * P] for a in range(HP)],
                           [p_s[:, j, a * P:(a + 1) * P] for a in range(HP)], pt_done)

            def values(b, j):
                pe.wait_ge(pt_ready, TPB * b + j + 1)
                for a in range(HP):
                    at = (j * HP + a) * VW
                    last = mm(bank_o[:, at:at + VW], p_t[:, j, a * P:(a + 1) * P], v_blk[:, a, :])
                return last

            def body(b):
                s0, s1, s2, s3, s4 = stages(b)
                if s1:
                    transpose_x(b + 1)
                if s2:
                    transpose_p(b, 0)
                if s1:
                    project(b + 1)
                if s2:
                    transpose_p(b, 1)
                if s3:
                    transpose_x2(b - 1)
                if s2:
                    gate_up_weights(b + 1, (0, 1, 2, 3))
                if s3:
                    logits(b - 1)
                if s2:
                    pe.wait_ge(vblk_ready, 2 * (b + 1))
                    pe.wait_ge(x2_done, b)
                    values(b, 0)
                    values(b, 1).then_inc(pv_done, 1)
                    down_weights(b + 1)
                if s1:
                    scores(b + 1)
                if s2:
                    pe.wait_ge(o_ready, b + 1)
                    o_flat = o_s[:, :, :].rearrange("p h d -> p (h d)")
                    transposes([bank_o[:, t * P:(t + 1) * P] for t in range(TPB)],
                               [o_flat[:, t * P:(t + 1) * P] for t in range(TPB)], ot_done)
                    pe.wait_ge(ot_ready, b + 1)
                    for t in range(TPB):
                        last = mm(bank_o[:, TOK + t * D:TOK + (t + 1) * D], o_t[:, t * P:(t + 1) * P], wo_s[:, :])
                    last.then_inc(wo_done, 1)
                if s3:
                    count_choosers(b - 1)

            pe.wait_ge(made, MADE)
            pe.wait_ge(gate_in, 16)
            transposes([bank_r[:, 0:E]], [gw_raw[:, :]], gwt_done)
            pe.wait_ge(bvrep_ready, 1)
            mm(bank_o[:, 0:D], bv_rep[:, :], wo_s[:, :]).then_inc(bias_done, 1)
            gate_up_weights(0, (0, 2))
            pe.wait_ge(wgu_ready, 2)
            transposes([bank_w[:, 0:P]], [raw_w[:, 4, :]], wd_done)
            pe.wait_ge(gwt_ready, 1)
            pe.wait_ge(bias_ready, 1)
            loop, last = phase1(body)
            with pe.Fori(loop.start, loop.stop) as b:
                body(b)
            for b in last:
                body(b)

            def page_x(i, j):
                pe.wait_ge(page_in[j], 16 * (i + 1))
                transposes([xt_ps[j % 2][:, g * P:(g + 1) * P] for g in range(QUAD)], [pg[j][:, g, 0:D] for g in range(QUAD)],
                           pxt_done)

            def experts(j):
                v = nc.values_load(expert_i[j][0:1, 0:1], engines=(mybir.EngineType.PE,), min_val=0, max_val=E ** QUAD - 1,
                                   skip_runtime_bounds_check_because="it packs four results of max_index over E experts")
                return [(v // E ** g) % E for g in range(QUAD)]

            def gate_up(q, j, e):
                pe.wait_ge(pxt_ready, q + 1)
                for g in range(QUAD):
                    last = mm(gu_ps[j % 2][:, g * P:(g + 1) * P], pxt[j % 2][:, g * P:(g + 1) * P],
                              w_gu[:, bass.ds(e[g], 1), :].rearrange("p e i -> p (e i)"))
                last.then_inc(gu_done, 1)

            def transpose_h(q, j, first):
                pe.wait_ge(h_ready, q + 1)
                if not first:
                    pe.wait_ge(ht_ready, q)
                transposes([bank_q[:, g * P:(g + 1) * P] for g in range(QUAD // 2)],
                           [h_s[j % 2][:, 2 * g:2 * g + 2, :].rearrange("p g i -> p (g i)") for g in range(QUAD // 2)], ht_done)

            def down(q, j, e, first):
                pe.wait_ge(ht_ready, q + 1)
                if not first:
                    pe.wait_ge(y_ready, q)
                for g in range(QUAD):
                    last = mm(bank_o[:, g * D:(g + 1) * D], h_t[j % 2][:, g, :],
                              w_d[:, bass.ds(e[g], 1), :].rearrange("p e h -> p (e h)"))
                last.then_inc(y_done, 1)

            def quads(i, first, last):
                cols = bass.ds(i * TOK, TOK)
                q = i * SLOTS
                e = {0: experts(0)}
                for j in range(SLOTS):
                    gate_up(q + j, j, e[j])
                    if j == 0:
                        mm(bank_r[:, 0:TOK], sg_t[:, :], x_all[:, cols]).then_inc(sh_gate, 1)
                    if j == 1:
                        pe.wait_ge(sh_silu, i + 1)
                        mm(bank_r[:, TOK:2 * TOK], su_t[:, :], x_all[:, cols]).then_inc(sh_up, 1)
                    if j + 1 < SLOTS:
                        page_x(i, j + 1)
                    elif not last:
                        page_x(i + 1, 0)
                    if j > 0:
                        down(q + j - 1, j - 1, e[j - 1], first and j == 1)
                    if j + 1 < SLOTS or not last:
                        pe.wait_ge(packed, q + j + 2)
                    transpose_h(q + j, j, first and j == 0)
                    if j + 1 < SLOTS:
                        e[j + 1] = experts(j + 1)
                pe.wait_ge(sh_ready, i + 1)
                if not first:
                    pe.wait_ge(sh_added, i)
                for t in range(TPB):
                    end = mm(bank_w[:, t * D:(t + 1) * D], sh_h[:, t * P:(t + 1) * P], sd_t[:, :])
                end.then_inc(sh_done, 1)
                down(q + SLOTS - 1, SLOTS - 1, e[SLOTS - 1], False)

            pe.wait_ge(pt_ready, TPB * B)
            pe.wait_ge(x2_done, B)
            pe.wait_ge(ranks_ready, B)
            pe.wait_ge(wd_ready, 2 * (B + 1))
            pe.wait_ge(packed, 1)
            page_x(0, 0)
            quads(0, True, False)
            with pe.Fori(1, NQ // SLOTS - 1) as i:
                quads(i, False, False)
            quads(NQ // SLOTS - 1, False, True)


INPUTS = ["x", "ctx_768", "L0_xattn_Wq", "L0_xattn_bq", "L0_xattn_Wk", "L0_xattn_bk", "L0_xattn_Wv", "L0_xattn_bv",
          "L0_xattn_Wo", "L0_xattn_bo", "L0_ffn_gate_w", "L0_ffn_gate_bias", "L0_ffn_eg_w", "L0_ffn_eu_w",
          "L0_ffn_ed_w", "L0_ffn_sg_w", "L0_ffn_su_w", "L0_ffn_sd_w"]


def kernel(**inputs):
    import concourse.bacc as bacc
    from concourse.bass_utils import run_bass_kernel_spmd

    nc = bacc.Bacc("TRN2", target_bir_lowering=False, num_devices=1)
    arrays, args = {}, []
    for name in INPUTS:
        a = np.ascontiguousarray(inputs[name])
        arrays[f"in_{name}"] = a
        args.append(nc.dram_tensor(f"in_{name}", a.shape, mybir.dt.from_np(a.dtype), kind="ExternalInput").ap())
    args.append(nc.dram_tensor("out_x", (B, TOK, D), F32, kind="ExternalOutput").ap())
    args.append(nc.dram_tensor("pages", (PAGES * P, PC), F32, kind="Internal").ap())
    args.append(nc.dram_tensor("results", (B * TOK * TOPK, D), F32, kind="Internal").ap())
    build(nc, *args)
    return run_bass_kernel_spmd(nc, [arrays], core_ids=[0]).results[0]["out_x"]
```

```python
from contextlib import ExitStack

import numpy as np

import concourse.bass as bass
from concourse import mybir

F32 = mybir.dt.float32
BF16 = mybir.dt.bfloat16
I32 = mybir.dt.int32
U32 = mybir.dt.uint32
ALU = mybir.AluOpType
ACT = mybir.ActivationFunctionType
AX = mybir.AxisListType

P = 128
B = 16
TPB = 2
TOK = TPB * P
KV = 64
D = 128
DC = 96
NH = 16
DH = D // NH
HP = NH // 2
VW = 2 * (DH + 1)
E = 64
INTER = 64
G = 8
TOPK = 6
QUAD = 4
SLOTS = 4
PAGES = E + B * TOK * TOPK // P
NQ = PAGES // QUAD
CODE, EXPERT, WEIGHT = D, D + 1, D + 2
PC = D + 3
FILL = B * TOK * TOPK // P // B
FIRST_FILL = PAGES % FILL
FILLS = PAGES // FILL
FILLS_AHEAD = 1 + (E - FIRST_FILL) // FILL + 1
NO_CODE = 1000000
SCALE = 1.0 / float(np.sqrt(DH))
EPS = 1e-5
BIG = 3.0e38
TAKEN = -1.0e38
ROUTE_STEPS = 20
PLACE_STEPS = 21
NCONST = 9
MADE = 12


def build(nc, x, ctx_rows, wq, bq, wk, bk, wv, bv, wo, bo, gate_w, gate_bias, eg, eu, ed, sg, su, sd, out, pages, results):
    with ExitStack() as ctx:
        def sb(name, shape, dt=F32):
            return ctx.enter_context(nc.sbuf_tensor(name, shape, dt))

        def ps(name, cols):
            return ctx.enter_context(nc.psum_tensor(name, [P, cols], F32))

        def sem(name):
            return ctx.enter_context(nc.semaphore(name))

        bank_s = [ps(f"bank_s{j}", 1024) for j in range(TPB)]
        bank_q = ps("bank_q", 512)
        bank_o = ps("bank_o", 512)
        bank_r = ps("bank_r", 512)
        bank_w = ps("bank_w", 512)
        xt_ps = [bank_s[0][:, i * 512:(i + 1) * 512] for i in range(2)]
        gu_ps = [bank_s[1][:, i * 512:(i + 1) * 512] for i in range(2)]

        w_gu = sb("w_gu", [P, E, 2 * INTER])
        w_d = sb("w_d", [INTER, E, D])
        sg_t = sb("sg_t", [D, P])
        su_t = sb("su_t", [D, P])
        sd_t = sb("sd_t", [P, D])
        x_all = sb("x_all", [P, B * TOK])
        xb = sb("xb", [P, B * TPB, D])
        ident = sb("ident", [P, P])
        before = sb("before", [P, P])
        before_h = sb("before_h", [P, P], BF16)
        ones_h = sb("ones_h", [P, P], BF16)
        head_mask = sb("head_mask", [P, NH])
        iota_e = sb("iota_e", [P, E])
        zeros = sb("zeros", [P, E])
        wq_s = sb("wq_s", [D, D])
        wk_s = sb("wk_s", [DC, D])
        wv_s = sb("wv_s", [DC, D])
        wo_s = sb("wo_s", [D, D])
        bq_s = sb("bq_s", [D, 1])
        bqs_s = sb("bqs_s", [D, 1])
        bk_s = sb("bk_s", [D, 1])
        bv_s = sb("bv_s", [D, 1])
        bv_rep = sb("bv_rep", [D, P])
        bo_s = sb("bo_s", [P, D])
        bias_s = sb("bias_s", [P, D])
        gw_t = sb("gw_t", [D, E])
        gw_raw = sb("gw_raw", [E, D])
        gb_s = sb("gb_s", [P, E])
        eps_s = sb("eps_s", [P, 2 * TPB])
        minus_half = sb("minus_half", [P, 2 * TPB])
        empty = sb("empty", [P, FILL, PC])
        ctx_s = sb("ctx_s", [P, DC])
        raw_w = sb("raw_w", [P, 6, P])
        st1 = sb("st1", [P, TPB, 6])
        mv = sb("mv", [P, 2 * TPB, 2])
        mv1, mv2 = mv[:, 0:TPB, :], mv[:, TPB:, :]
        ve = sb("ve", [P, 2 * TPB])
        rstd = [sb(f"rstd{i}", [P, 2 * TPB]) for i in range(2)]
        st2 = sb("st2", [P, TPB, 6])
        xn = sb("xn", [P, TPB, D])
        xn_t = sb("xn_t", [P, TOK])
        ctx_t = sb("ctx_t", [DC, P])
        q_t = sb("q_t", [P, TOK])
        k_t = sb("k_t", [P, KV])
        k_exp = sb("k_exp", [P, NH, KV])
        v_all = sb("v_all", [P, B, HP, VW])
        mx = sb("mx", [P, TPB, NH])
        minus_max = sb("minus_max", [P, NH])
        p_s = sb("p_s", [P, TPB, NH * KV])
        p_t = sb("p_t", [P, TPB, HP * P])
        rsum = sb("rsum", [P, TPB * NH])
        o_s = sb("o_s", [P, TPB * NH, DH])
        o_t = sb("o_t", [P, TOK])
        xn2 = [sb(f"xn2_{i}", [P, TPB, D]) for i in range(2)]
        x2_t = sb("x2_t", [P, TOK])
        sig = sb("sig", [P, TPB, E])
        score = sb("score", [P, TPB, E])
        grp = sb("grp", [P, TPB, G + 4])
        grp_top = sb("grp_top", [P, TPB, 8])
        grp_rep = sb("grp_rep", [P, TPB, G + 4])
        msk = sb("msk", [P, TPB, E + 2])
        msk_rep = sb("msk_rep", [P, TPB, E + 2])
        top = sb("top", [P, TPB, 8])
        top_at = sb("top_at", [P, TPB, 8], U32)
        wsum = sb("wsum", [P, TPB])
        weight = sb("weight", [P, TPB, TOPK])
        chosen = sb("chosen", [P, TPB, E], BF16)
        ranks = sb("ranks", [P, 2, TPB, E])
        fill = sb("fill", [P, E])
        base2 = sb("base2", [P, E])
        next_page = [sb(f"next_page{t}", [P, E]) for t in range(TPB)]
        rank = sb("rank", [P, E])
        filled_to = sb("filled_to", [P, E])
        opens = sb("opens", [P, E])
        jump = sb("jump", [P, E])
        jumped = sb("jumped", [P, E])
        row = sb("row", [P, E])
        move = sb("move", [P, E])
        picked = sb("picked", [P, TOPK, E])
        expert_f = [sb(f"expert_f{t}", [P, TOPK]) for t in range(TPB)]
        place = [sb(f"place{t}", [P, TOPK]) for t in range(TPB)]
        place_i = [sb(f"place_i{t}", [P, TOPK], I32) for t in range(TPB)]
        payload = [sb(f"payload{t}", [P, TOPK, PC]) for t in range(TPB)]
        pg = [sb(f"pg{j}", [P, QUAD, PC]) for j in range(SLOTS)]
        codes = [sb(f"codes{j}", [P, QUAD], I32) for j in range(SLOTS)]
        scales = [sb(f"scales{j}", [P, QUAD]) for j in range(SLOTS)]
        digit = sb("digit", [1, QUAD])
        digits = sb("digits", [1, QUAD])
        expert_i = [sb(f"expert_i{j}", [1, 1], I32) for j in range(SLOTS)]
        spare = sb("spare", [P, 1])
        y_s = [sb(f"y_s{j}", [P, QUAD, D]) for j in range(SLOTS)]
        pxt = [sb(f"pxt{j}", [P, QUAD * P]) for j in range(2)]
        s_act = sb("s_act", [P, QUAD, INTER])
        h_s = [sb(f"h_s{j}", [P, QUAD, INTER]) for j in range(2)]
        h_t = [sb(f"h_t{j}", [INTER, QUAD, P]) for j in range(2)]
        sh_act = sb("sh_act", [P, TOK])
        sh_h = sb("sh_h", [P, TOK])
        routed = sb("routed", [P, TPB, D])
        w_flat = w_gu[:, :, :].rearrange("p e i -> p (e i)")
        ys = [w_flat[:, j * 2 * TOPK * D:(j + 1) * 2 * TOPK * D].rearrange("p (t k h) -> p t k h", t=2, k=TOPK)
              for j in range(SLOTS)]

        x_first, x_rest, const_in, gate_in = sem("x_first"), sem("x_rest"), sem("const_in"), sem("gate_in")
        ctx_in, raw_in, prefilled = sem("ctx_in"), sem("raw_in"), sem("prefilled")
        values_zeroed = sem("values_zeroed")
        silu_loaded = sem("silu_loaded")
        zeroed, made, halved, empty_ready = sem("zeroed"), sem("made"), sem("halved"), sem("empty_ready")
        dve_made, bvrep_ready, bias_done, bias_ready = sem("dve_made"), sem("bvrep_ready"), sem("bias_done"), sem("bias_ready")
        gwt_done, gwt_ready = sem("gwt_done"), sem("gwt_ready")
        st1_done, mv1_done, st2_done, mv2_done = sem("st1_done"), sem("mv1_done"), sem("st2_done"), sem("mv2_done")
        ve_done, rstd_done = sem("ve_done"), sem("rstd_done")
        xc_ready, xn_ready, xt_done, xts_ready = sem("xc_ready"), sem("xn_ready"), sem("xt_done"), sem("xts_ready")
        qkv_done, k_ready, q_ready = sem("qkv_done"), sem("k_ready"), sem("q_ready")
        kexp_ready, vblk_ready = sem("kexp_ready"), sem("vblk_ready")
        negated = sem("negated")
        scores_done, mx_done, shifted, p_ready = sem("scores_done"), sem("mx_done"), sem("shifted"), sem("p_ready")
        pt_done, pt_ready, pv_done = sem("pt_done"), sem("pt_ready"), sem("pv_done")
        rsum_done, o_ready, ot_done, ot_ready = sem("rsum_done"), sem("o_ready"), sem("ot_done"), sem("ot_ready")
        wo_done, x2_done = sem("wo_done"), sem("x2_done")
        x2c_ready, xn2_ready, x2t_done, x2t_ready = sem("x2c_ready"), sem("xn2_ready"), sem("x2t_done"), sem("x2t_ready")
        logit_done, sig_ready, route, chosen_ready = sem("logit_done"), sem("sig_ready"), sem("route"), sem("chosen_ready")
        ranks_done, ranks_ready, placed = sem("ranks_done"), sem("ranks_ready"), sem("placed")
        payload_x, place_ready, code_ready, spared, digits_done, packed = sem("payload_x"), sem("place_ready"), sem("code_ready"), sem("spared"), sem("digits_done"), sem("packed")
        scattered = [sem(f"scattered{t}") for t in range(TPB)]
        wgu_done, wgu_ready, wd_done, wd_ready = sem("wgu_done"), sem("wgu_ready"), sem("wd_done"), sem("wd_ready")
        page_in = [sem(f"page_in{j}") for j in range(SLOTS)]
        y_out = [sem(f"y_out{j}") for j in range(SLOTS)]
        pxt_done, pxt_ready, gu_done, act_ready, h_ready = sem("pxt_done"), sem("pxt_ready"), sem("gu_done"), sem("act_ready"), sem("h_ready")
        ht_done, ht_ready, y_done, y_ready = sem("ht_done"), sem("ht_ready"), sem("y_done"), sem("y_ready")
        sh_gate, sh_silu, sh_up, sh_ready, sh_done, sh_added = (sem("sh_gate"), sem("sh_silu"), sem("sh_up"), sem("sh_ready"),
                                                                sem("sh_done"), sem("sh_added"))
        ys_in = [sem(f"ys_in{j}") for j in range(SLOTS)]
        empty_zeroed, added, summed, out_done = sem("empty_zeroed"), sem("added"), sem("summed"), sem("out_done")

        x_v = x.rearrange("b (t p) h -> p (b t) h", p=P)
        out_v = out.rearrange("b (t p) h -> p (b t) h", p=P)
        eg_v = eg.rearrange("(w j a) i h -> w (a i) j h", j=2, a=2)
        eu_v = eu.rearrange("(w j a) i h -> w (a i) j h", j=2, a=2)
        ed_v = ed.rearrange("(w e) h i -> w h e i", e=4)
        fill_v = pages[FIRST_FILL * P:PAGES * P, :].rearrange("(k p r) c -> k p (r c)", p=P, r=FILL)
        quad_v = pages.rearrange("(q g p) c -> q p g c", g=QUAD, p=P)
        ys_v = results.rearrange("(t p k) h -> p t k h", p=P, k=TOPK)

        def line(ap):
            return ap.rearrange("(a n) -> a n", a=1)

        def col(ap):
            return ap.rearrange("(p a) -> p a", a=1)

        def stages(b):
            if not isinstance(b, int):
                return True, True, True, True, True, True
            return 0 <= b + 2 < B, b + 1 < B, 0 <= b < B, 1 <= b <= B, 2 <= b <= B + 1, 3 <= b

        def phase1(body):
            for b in range(-1, 4):
                body(b, b % 2)
            return range(4, B - 4, 2), range(B - 4, B + 3)

        block = ctx.enter_context(nc.Block())

        @block.sync
        def _(sp):
            def load_ctx(b):
                for half in range(2):
                    sp.dma_start(ctx_s[half * KV:(half + 1) * KV, :], ctx_rows[bass.ds(b, 1), :, :].rearrange(
                        "a s d -> (a s) d")).then_inc(ctx_in, 16)

            def load_raw(w):
                sp.dma_start(raw_w[:, 0:2, :], eg_v[bass.ds(w, 1), :, :, :].rearrange(
                    "a p j h -> (a p) j h")).then_inc(raw_in, 16)
                sp.dma_start(raw_w[:, 2:4, :], eu_v[bass.ds(w, 1), :, :, :].rearrange(
                    "a p j h -> (a p) j h")).then_inc(raw_in, 16)
                sp.dma_start(raw_w[:, 4:6, :].rearrange("p j (e i) -> p (j e) i", e=2), ed_v[
                    bass.ds(w, 1), :, :, :].rearrange("a h e i -> (a h) e i")).then_inc(raw_in, 16)

            def prefill(k):
                sp.wait_ge(prefilled, 16 * (k + 1))
                sp.dma_start(fill_v[bass.ds(k, 1), :, :].rearrange("k p c -> (k p) c"),
                             empty[:, :, :].rearrange("p r c -> p (r c)")).then_inc(prefilled, 16)

            def load_batch(b):
                sp.wait_ge(xt_done, b + 1)
                load_ctx(b + 1)
                sp.wait_ge(wd_done, b + 1)
                load_raw(b)

            sp.dma_start(xb[:, 0:TPB, :], x_v[:, 0:TPB, :]).then_inc(x_first, 16)
            load_ctx(0)
            for dst, src in ((wq_s, wq), (wk_s, wk), (wv_s, wv), (bq_s, col(bq)), (bk_s, col(bk)), (bv_s, col(bv)), (wo_s, wo)):
                sp.dma_start(dst[:, :], src).then_inc(const_in, 16)
            for dst, src, n in ((bo_s, bo, D), (gb_s, gate_bias, E)):
                sp.dma_start(dst[:, :], line(src).to_broadcast([P, n])).then_inc(const_in, 16)
            sp.dma_start(gw_raw[:, :], gate_w).then_inc(gate_in, 16)
            sp.dma_start(xb[:, TPB:, :], x_v[:, TPB:, :]).then_inc(x_rest, 16)
            sp.dma_start(raw_w[:, 0, :], sg).then_inc(raw_in, 16)
            sp.dma_start(raw_w[:, 2, :], su).then_inc(raw_in, 16)
            sp.dma_start(raw_w[:, 4, :], sd).then_inc(raw_in, 16)
            sp.wait_ge(empty_ready, 1)
            sp.dma_start(pages[0:FIRST_FILL * P, :].rearrange("(p r) c -> p (r c)", p=P),
                         empty[:, 0:FIRST_FILL, :].rearrange("p r c -> p (r c)")).then_inc(prefilled, 16)
            for b in range(4):
                load_batch(b)
                prefill(2 * b)
                prefill(2 * b + 1)
            with sp.Fori(4, B - 1) as b:
                load_batch(b)
                prefill(b + 4)
            sp.wait_ge(wd_done, B)
            load_raw(B - 1)
            prefill(FILLS - 2)
            prefill(FILLS - 1)
            for t in range(TPB):
                sp.wait_ge(scattered[t], 16 * TOPK * B)

            def load_quads(i, first):
                for j in range(SLOTS):
                    q = i * SLOTS + j
                    if not first:
                        sp.wait_ge(code_ready, q - SLOTS + 1)
                    sp.dma_start(pg[j][:, :, :], quad_v[bass.ds(q, 1), :, :, :].rearrange(
                        "a p g c -> (a p) g c")).then_inc(page_in[j], 16)

            load_quads(0, True)
            with sp.Fori(1, NQ // SLOTS) as i:
                load_quads(i, False)

            for j in range(SLOTS):
                sp.wait_ge(y_out[j], 16 * QUAD * NQ // SLOTS)
            sp.wait_ge(gu_done, NQ)

            def load_results(i, first):
                for j in range(SLOTS):
                    n = i * SLOTS + j
                    if not first:
                        sp.wait_ge(summed, n - SLOTS + 1)
                    sp.dma_start(ys[j], ys_v[:, bass.ds(n * 2, 2), :, :]).then_inc(ys_in[j], 16)

            load_results(0, True)
            with sp.Fori(1, B // SLOTS) as i:
                load_results(i, False)
            sp.wait_ge(out_done, 16 * B)

        @block.gpsimd
        def _(pool):
            pool.memset(ident[:, :], 0.0).then_inc(zeroed, 1)
            pool.memset(before[:, :], 1.0).then_inc(zeroed, 1)
            pool.memset(head_mask[:, :], 1.0).then_inc(zeroed, 1)
            pool.memset(zeros[:, :], 0.0).then_inc(made, 1)
            pool.memset(eps_s[:, :], EPS).then_inc(made, 1)
            pool.memset(minus_half[:, :], -0.5).then_inc(made, 1)
            pool.memset(grp[:, :, G:], BIG).then_inc(made, 1)
            pool.memset(msk[:, :, E:], BIG).then_inc(made, 1)
            pool.wait_ge(zeroed, 3)
            pool.affine_select(out=ident[:, :], in_=ident[:, :], compare_op=ALU.not_equal, fill=1.0, base=0,
                               pattern=[[-1, P]], channel_multiplier=1).then_inc(made, 1)
            pool.affine_select(out=before[:, :], in_=before[:, :], compare_op=ALU.is_ge, fill=0.0, base=-1,
                               pattern=[[1, P]], channel_multiplier=-1).then_inc(made, 1)
            pool.affine_select(out=head_mask[:, :], in_=head_mask[:, :], compare_op=ALU.is_ge, fill=0.0, base=0,
                               pattern=[[-DH, NH]], channel_multiplier=1).then_inc(halved, 1)
            pool.wait_ge(halved, 1)
            pool.affine_select(out=head_mask[:, :], in_=head_mask[:, :], compare_op=ALU.is_ge, fill=0.0, base=DH - 1,
                               pattern=[[DH, NH]], channel_multiplier=-1).then_inc(made, 1)
            pool.iota(iota_e[:, :], [[1, E]], base=0, channel_multiplier=0,
                      allow_small_or_imprecise_dtypes=True).then_inc(made, 1)
            pool.iota(base2[:, :], [[P, E]], base=2 * P, channel_multiplier=0,
                      allow_small_or_imprecise_dtypes=True).then_inc(made, 1)
            for t in range(TPB):
                pool.iota(payload[t][:, :, CODE].bitcast(I32), [[1, TOPK]], base=t * P * TOPK - TOK * TOPK,
                          channel_multiplier=TOPK).then_inc(made, 1)

            pool.memset(v_all[:, :, :, :], 0.0).then_inc(values_zeroed, 1)

            def inverse_deviations(b, side, first, after):
                part = slice(first, after)
                pool.tensor_tensor(ve[:, part], mv[:, part, 1], eps_s[:, part], ALU.add).then_inc(ve_done, 1)
                pool.wait_ge(ve_done, b + 3)
                pool.tensor_tensor(rstd[side][:, part], ve[:, part], minus_half[:, part], ALU.pow).then_inc(rstd_done, 1)

            def centre(n, dst, part, centred):
                pool.tensor_tensor(dst[:, :, :], xb[:, bass.ds(TPB * n, TPB), :], mv[:, part, 0:1].to_broadcast([P, TPB, D]),
                                   ALU.subtract).then_inc(centred, 1)

            of_x, of_x2 = slice(0, TPB), slice(TPB, 2 * TPB)

            def expand_k(n):
                pool.wait_ge(k_ready, n + 1)
                pool.tensor_tensor(k_exp[:, :, :], k_t[:, :].unsqueeze(1).to_broadcast([P, NH, KV]),
                                   head_mask[:, :].unsqueeze(2).to_broadcast([P, NH, KV]),
                                   ALU.mult).then_inc(kexp_ready, 1)

            def wait_payload(n, t):
                pool.wait_ge(place_ready, TPB * n + t + 1)
                pool.wait_ge(payload_x, TPB * n + t + 1)
                pool.wait_ge(prefilled, 16 * (n + FILLS_AHEAD))
                pool.wait_ge(spared, TPB * n + t)
                pool.tensor_tensor(spare[:, :], zeros[:, 0:1], zeros[:, 0:1], ALU.add).then_inc(spared, 1)

            def scatter(t, ks=range(TOPK)):
                for k in ks:
                    pool.indirect_dma_start(out=pages[:, :], out_offset=bass.IndirectOffsetOnAxis(
                        ap=place_i[t][:, k:k + 1], axis=0), in_=payload[t][:, k, :], in_offset=None,
                        bounds_check=PAGES * P - 1, oob_is_err=False).then_inc(scattered[t], 16)

            def body(b, side):
                s0, s1, s2, so, s3, s4 = stages(b)
                if s3:
                    pool.wait_ge(mv2_done, TPB * (b - 1))
                    if not isinstance(b, int) or b >= 4:
                        pool.wait_ge(payload_x, TPB * (b - 3))
                    centre(b - 2, xn2[side], of_x2, x2c_ready)
                if s0:
                    pool.wait_ge(mv1_done, TPB * (b + 3))
                    pool.wait_ge(xt_done, b + 2)
                if s0 or s3:
                    inverse_deviations(b, side, 0 if s0 else TPB, 2 * TPB if s3 else TPB)
                if s3:
                    pool.wait_ge(rstd_done, b + 3)
                    pool.wait_ge(x2c_ready, b - 1)
                    pool.tensor_tensor(xn2[side][:, :, :], xn2[side][:, :, :],
                                       rstd[side][:, of_x2].unsqueeze(2).to_broadcast([P, TPB, D]), ALU.mult).then_inc(xn2_ready, TPB)
                if s0:
                    centre(b + 2, xn, of_x, xc_ready)
                if s1:
                    expand_k(b + 1)
                if s4:
                    wait_payload(b - 3, 0)
                    scatter(0)
                    wait_payload(b - 3, 1)
                    scatter(1)

            pool.wait_ge(mv1_done, TPB)
            inverse_deviations(-2, 0, 0, TPB)
            centre(0, xn, of_x, xc_ready)
            loop, last = phase1(body)
            with pool.Fori(loop.start, loop.stop, loop.step) as b:
                body(b, 0)
                body(b + 1, 1)
            for b in last:
                body(b, b % 2)

            def quads(i):
                for j in range(SLOTS):
                    q = i * SLOTS + j
                    pool.wait_ge(code_ready, q + 1)
                    pool.wait_ge(y_ready, q + 1)
                    pool.wait_ge(spared, q + TPB * B)
                    pool.tensor_tensor(spare[:, :], zeros[:, 0:1], zeros[:, 0:1], ALU.add).then_inc(spared, 1)
                    for g in range(QUAD):
                        pool.indirect_dma_start(out=results[:, :], out_offset=bass.IndirectOffsetOnAxis(
                            ap=codes[j][:, g:g + 1], axis=0), in_=y_s[j][:, g, :], in_offset=None,
                            bounds_check=B * TOK * TOPK - 1, oob_is_err=False).then_inc(y_out[j], 16)

            with pool.Fori(0, NQ // SLOTS) as i:
                quads(i)

        @block.scalar
        def _(act):
            def copy(dst, src):
                return act.activation(dst, src, ACT.Copy)

            def transposed_x(n):
                act.wait_ge(xt_done, n + 1)
                copy(xn_t[:, :], bank_q[:, 0:TOK]).then_inc(xts_ready, 1)
                copy(ctx_t[:, :], bank_q[0:DC, TOK:TOK + P]).then_inc(xts_ready, 1)

            def evacuate_qk(n):
                act.wait_ge(qkv_done, n + 1)
                act.activation(k_t[:, :], bank_q[:, TOK:TOK + KV], ACT.Identity, bias=bk_s[:, 0:1]).then_inc(k_ready, 1)
                act.activation(q_t[:, :], bank_q[:, 0:TOK], ACT.Identity, bias=bqs_s[:, 0:1], scale=SCALE).then_inc(q_ready, 1)

            def transposed_x2(n):
                act.wait_ge(x2t_done, n + 1)
                copy(x2_t[:, :], bank_r[:, 0:TOK]).then_inc(x2t_ready, 1)
                copy(x_all[:, bass.ds(n * TOK, TOK)], bank_r[:, 0:TOK]).then_inc(x2t_ready, 1)

            def exps(b, j):
                if j == 0:
                    act.wait_ge(shifted, b + 1)
                    act.activation(p_s[:, j, :], p_s[:, j, :], ACT.Exp).then_inc(p_ready, 1)
                else:
                    act.wait_ge(negated, b + 1)
                    for h in range(NH):
                        part = slice(h * KV, (h + 1) * KV)
                        last = act.activation(p_s[:, j, part], bank_s[j][:, part], ACT.Exp, bias=minus_max[:, h:h + 1])
                    last.then_inc(p_ready, 1)

            def copy_pt(b, j):
                act.wait_ge(pt_done, TPB * b + j + 1)
                copy(p_t[:, j, :], bank_s[j][:, :]).then_inc(pt_ready, 1)

            def sigmoid_exp(n):
                act.wait_ge(logit_done, n + 1)
                act.activation(sig[:, :, :].rearrange("p t e -> p (t e)"), bank_r[:, TOK:TOK + TPB * E], ACT.Exp,
                               scale=-1.0).then_inc(sig_ready, 1)

            def evacuate_v(n):
                for h in range(2):
                    rows = slice(h * KV, (h + 1) * KV)
                    copy(v_all[rows, bass.ds(n, 1), :, h * (DH + 1):h * (DH + 1) + DH].rearrange("p b a d -> p (b a) d"),
                         bank_q[rows, TOK + KV:TOK + KV + D].rearrange("p (a h d) -> p a h d", h=2, d=DH)[
                             :, :, h, :]).then_inc(vblk_ready, 1)

            def scale_x(n, side):
                act.wait_ge(xc_ready, n + 1)
                for t in range(TPB):
                    act.activation(xn[:, t, :], xn[:, t, :], ACT.Identity, scale=rstd[side][:, t:t + 1]).then_inc(xn_ready, 1)

            def copy_ranks(n):
                act.wait_ge(ranks_done, n + 1)
                act.wait_ge(placed, PLACE_STEPS * TPB * n)
                copy(ranks[:, :, :, :].rearrange("p a t e -> p (a t e)"), bank_r[:, 0:TOK]).then_inc(ranks_ready, 1)

            def fill_payload(n, side, t):
                act.wait_ge(xn2_ready, TPB * n + t + 1)
                act.wait_ge(scattered[t], 16 * TOPK * n)
                copy(payload[t][:, :, 0:D], xn2[side][:, t, :].unsqueeze(1).to_broadcast([P, TOPK, D])).then_inc(payload_x, 1)

            def gate_up_weights(w):
                act.wait_ge(wgu_done, w + 2)
                copy(w_gu[:, bass.ds(4 * w, 4), :].rearrange("p e (u i) -> p u e i", u=2),
                     bank_w[:, :].rearrange("p (u e i) -> p u e i", u=2, e=4)).then_inc(wgu_ready, 1)

            def down_weights(w):
                act.wait_ge(wd_done, w + 2)
                for a in range(2):
                    copy(w_d[:, bass.ds(4 * w, 4), :].rearrange("p (j a) h -> p j a h", a=2)[:, :, a, :],
                         bank_w[a * INTER:(a + 1) * INTER, 0:2 * P].rearrange("p (j h) -> p j h", j=2)).then_inc(wd_ready, 1)

            def body(b, side):
                s0, s1, s2, so, s3, s4 = stages(b)
                if s1:
                    transposed_x(b + 1)
                if s4:
                    copy_ranks(b - 3)
                    fill_payload(b - 3, 1 - side, 0)
                if s2:
                    exps(b, 0)
                if s1:
                    evacuate_qk(b + 1)
                if s2:
                    exps(b, 1)
                if s3:
                    transposed_x2(b - 2)
                if so:
                    act.wait_ge(ot_done, b)
                    copy(o_t[:, :], bank_o[:, 0:TOK]).then_inc(ot_ready, 1)
                if s3:
                    sigmoid_exp(b - 2)
                if s2:
                    copy_pt(b, 0)
                if s1:
                    evacuate_v(b + 1)
                if s4:
                    fill_payload(b - 3, 1 - side, 1)
                if s2:
                    copy_pt(b, 1)
                if s0:
                    scale_x(b + 2, side)
                if s2:
                    gate_up_weights(b)
                    down_weights(b)

            act.wait_ge(gwt_done, 1)
            copy(gw_t[:, :], bank_r[:, 0:E]).then_inc(gwt_ready, 1)
            scale_x(0, 0)
            act.wait_ge(dve_made, 2)
            act.wait_ge(const_in, 16 * NCONST)
            act.wait_ge(wgu_done, 1)
            copy(sg_t[:, :], bank_w[:, 0:P]).then_inc(wgu_ready, 1)
            copy(su_t[:, :], bank_w[:, P:2 * P]).then_inc(wgu_ready, 1)
            act.wait_ge(wd_done, 1)
            copy(sd_t[:, :], bank_w[:, 0:P]).then_inc(wd_ready, 2)
            loop, last = phase1(body)
            with act.Fori(loop.start, loop.stop, loop.step) as b:
                body(b, 0)
                body(b + 1, 1)
            for b in last:
                body(b, b % 2)

            def page_x(q, j):
                act.wait_ge(pxt_done, q + 1)
                copy(pxt[j % 2][:, :], xt_ps[j % 2]).then_inc(pxt_ready, 1)

            def page_result(i, j, first):
                act.wait_ge(y_done, i * SLOTS + j + 1)
                if not first:
                    act.wait_ge(y_out[j], 16 * QUAD * i)
                act.wait_ge(code_ready, i * SLOTS + j + 1)
                for g in range(QUAD):
                    scaled = act.activation(y_s[j][:, g, :], bank_o[:, g * D:(g + 1) * D], ACT.Identity,
                                            scale=scales[j][:, g:g + 1])
                scaled.then_inc(y_ready, 1)

            def quads(i, first, last):
                for j in range(SLOTS):
                    q = i * SLOTS + j
                    act.wait_ge(gu_done, q + 1)
                    if not (first and j == 0):
                        act.wait_ge(h_ready, q)
                    act.activation(s_act[:, :, :], gu_ps[j % 2].rearrange("p (g u i) -> p g u i", g=QUAD, u=2)[:, :, 0, :],
                                   ACT.Silu).then_inc(act_ready, 1)
                    if j == 0:
                        act.wait_ge(sh_gate, i + 1)
                        act.activation(sh_act[:, :], bank_r[:, 0:TOK], ACT.Silu).then_inc(sh_silu, 1)
                    if j + 1 < SLOTS:
                        page_x(q + 1, j + 1)
                    elif not last:
                        page_x(q + 1, 0)
                    if j > 0:
                        page_result(i, j - 1, first)
                page_result(i, SLOTS - 1, first)

            act.activation(sh_act[:, 0:1], zeros[:, 0:1], ACT.Silu).then_inc(silu_loaded, 1)
            act.wait_ge(silu_loaded, 1)
            page_x(0, 0)
            quads(0, True, False)
            with act.Fori(1, NQ // SLOTS - 1) as i:
                quads(i, False, False)
            quads(NQ // SLOTS - 1, False, True)

            def store(n):
                act.wait_ge(summed, n + 1)
                act.dma_start(out_v[:, bass.ds(n * TPB, TPB), :], xb[:, bass.ds(n * TPB, TPB), :]).then_inc(out_done, 16)

            with act.Fori(0, B) as n:
                store(n)

        @block.vector
        def _(dve):
            dve.memset(empty[:, :, :], 0.0).then_inc(empty_zeroed, 1)
            dve.wait_ge(empty_zeroed, 1)
            dve.memset(empty[:, :, CODE:CODE + 1].bitcast(I32), NO_CODE).then_inc(empty_ready, 1)
            dve.wait_ge(made, MADE)
            dve.memset(fill[:, :], 0.0)
            dve.memset(ones_h[:, :], 1.0)
            for g in range(QUAD):
                dve.memset(digit[:, g:g + 1], float(E ** g))
            dve.memset(next_page[1][:, :], float(E)).then_inc(dve_made, 1)

            def x_tile(i):
                return xb[:, bass.ds(i, 1), :].rearrange("p t h -> p (t h)")

            def stats(n, t, st, st_done):
                dve.bn_stats(st[:, t, :], x_tile(TPB * n + t)).then_inc(st_done, 1)

            def aggregate(st, mv, mv_done):
                for t in range(TPB):
                    dve.bn_aggr(mv[:, t, :], st[:, t, :]).then_inc(mv_done, 1)


            def maxima(b, j):
                dve.wait_ge(scores_done, TPB * b + j + 1)
                dve.tensor_reduce(mx[:, j, :], bank_s[j][:, :].rearrange("p (h k) -> p h k", k=KV), AX.X,
                                  ALU.max).then_inc(mx_done, 1)

            def shift(b):
                dve.wait_ge(mx_done, TPB * b + 1)
                dve.tensor_tensor(p_s[:, 0, :].rearrange("p (h k) -> p h k", k=KV),
                                  bank_s[0][:, :].rearrange("p (h k) -> p h k", k=KV),
                                  mx[:, 0, :].unsqueeze(2).to_broadcast([P, NH, KV]), ALU.subtract).then_inc(shifted, 1)

            def negate(b):
                dve.wait_ge(mx_done, TPB * (b + 1))
                dve.tensor_scalar(minus_max[:, :], mx[:, 1, :], -1.0, None, ALU.mult).then_inc(negated, 1)

            def routing(n, fillers):
                at = {}

                def chained(name, ins):
                    at[name] = len(at) + 1
                    ins.then_inc(route, 1)

                def after(name):
                    dve.wait_ge(route, n * ROUTE_STEPS + at[name])

                def filler():
                    if fillers:
                        fillers.pop(0)()

                flat = lambda t: t[:, :, :].rearrange("p t e -> p (t e)")
                dve.wait_ge(sig_ready, n + 1)
                chained("one_more", dve.tensor_scalar(flat(sig), flat(sig), 1.0, None, ALU.add))
                filler()
                after("one_more")
                chained("sigmoid", dve.reciprocal(flat(score), flat(sig)))
                filler()
                after("sigmoid")
                chained("score", dve.tensor_tensor(score[:, :, :], score[:, :, :],
                                                   gb_s[:, :].unsqueeze(1).to_broadcast([P, TPB, E]), ALU.add))
                after("score")
                chained("groups", dve.tensor_reduce(grp[:, :, 0:G], score[:, :, :].rearrange("p t (g e) -> p t g e", g=G),
                                                    AX.X, ALU.max))
                after("groups")
                filler()
                for t in range(TPB):
                    chained(("top_groups", t), dve.max(grp_top[:, t, :], grp[:, t, :]))
                filler()
                after(("top_groups", 1))
                filler()
                for t in range(TPB):
                    chained(("kept", t), dve.match_replace(grp_rep[:, t, :], grp_top[:, t, :], grp[:, t, :], -BIG))
                for t in range(TPB):
                    after(("kept", t))
                    chained(("masked", t), dve.scalar_tensor_tensor(
                        out=msk[:, t, 0:E].rearrange("p (g e) -> p g e", g=G),
                        in0=grp_rep[:, t, 0:G].unsqueeze(2).to_broadcast([P, G, E // G]), scalar=TAKEN,
                        in1=score[:, t, :].rearrange("p (g e) -> p g e", g=G), op0=ALU.is_lt, op1=ALU.mult))
                filler()
                after(("masked", 1))
                filler()
                for t in range(TPB):
                    chained(("top", t), dve.max(top[:, t, :], msk[:, t, :]))
                after(("top", 1))
                chained("sum", dve.tensor_reduce(wsum[:, :], top[:, :, 8 - TOPK:8], AX.X, ALU.add))
                for t in range(TPB):
                    chained(("chosen", t), dve.match_replace(msk_rep[:, t, :], top[:, t, :], msk[:, t, :], -BIG))
                    chained(("index", t), dve.max_index(top_at[:, t, :], top[:, t, :], msk[:, t, :]))
                after("sum")
                chained("divisor", dve.tensor_scalar(wsum[:, :], wsum[:, :], 1e-8, None, ALU.add))
                after(("chosen", 1))
                dve.tensor_scalar(chosen[:, :, :], msk_rep[:, :, 0:E], TAKEN, None, ALU.is_lt).then_inc(chosen_ready, 1)
                after("divisor")
                chained("factor", dve.reciprocal(wsum[:, :], wsum[:, :]))
                after("factor")
                chained("weight", dve.tensor_tensor(weight[:, :, :], top[:, :, 8 - TOPK:8],
                                                    wsum[:, :].unsqueeze(2).to_broadcast([P, TPB, TOPK]), ALU.mult))
                assert len(at) == ROUTE_STEPS

            def find_places(n, t):
                at = {}
                base = PLACE_STEPS * (TPB * n + t)

                def chained(name, ins):
                    at[name] = len(at) + 1
                    ins.then_inc(placed, 1)

                def after(name):
                    dve.wait_ge(placed, base + at[name])

                dve.wait_ge(ranks_ready, n + 1)
                if not (isinstance(n, int) and n == 0 and t == 0):
                    dve.wait_ge(placed, base - TOPK)
                chained("filled_to", dve.tensor_tensor(filled_to[:, :], ranks[:, 1, t, :], fill[:, :], ALU.add))
                chained("rank", dve.tensor_tensor(rank[:, :], ranks[:, 0, t, :], fill[:, :], ALU.add))
                dve.wait_ge(scattered[t], 16 * TOPK * n)
                chained("expert", dve.tensor_copy(payload[t][:, :, EXPERT].bitcast(U32), top_at[:, t, 8 - TOPK:8]))
                chained("expert_f", dve.tensor_copy(expert_f[t][:, :], top_at[:, t, 8 - TOPK:8]))
                after("filled_to")
                chained("opens", dve.tensor_scalar(opens[:, :], filled_to[:, :], float(P), None, ALU.is_gt))
                chained("weight", dve.tensor_copy(payload[t][:, :, WEIGHT], weight[:, t, :]))
                code = payload[t][:, :, CODE].bitcast(I32)
                chained("code", dve.tensor_scalar(code, code, TOK * TOPK, None, ALU.add))
                after("rank")
                chained("row_here", dve.scalar_tensor_tensor(out=row[:, :], in0=rank[:, :], scalar=-2.0 * P, in1=base2[:, :],
                                                             op0=ALU.add, op1=ALU.add))
                after("opens")
                chained("pages", dve.tensor_tensor_scan(next_page[t][:, :], opens[:, :], zeros[:, :],
                                                        next_page[1 - t][:, E - 1:E], ALU.add, ALU.add))
                chained("fill", dve.scalar_tensor_tensor(out=fill[:, :], in0=opens[:, :], scalar=-float(P),
                                                         in1=filled_to[:, :], op0=ALU.mult, op1=ALU.add))
                after("pages")
                chained("jump", dve.scalar_tensor_tensor(out=jump[:, :], in0=next_page[t][:, :], scalar=float(P),
                                                         in1=base2[:, :], op0=ALU.mult, op1=ALU.subtract))
                after("jump")
                chained("jumped", dve.scalar_tensor_tensor(out=jumped[:, :], in0=rank[:, :], scalar=float(P), in1=jump[:, :],
                                                           op0=ALU.is_ge, op1=ALU.mult))
                chained("move", dve.scalar_tensor_tensor(out=move[:, :], in0=jump[:, :], scalar=float(P), in1=opens[:, :],
                                                         op0=ALU.add, op1=ALU.mult))
                after("jumped")
                chained("row", dve.tensor_tensor(row[:, :], row[:, :], jumped[:, :], ALU.add))
                after("move")
                chained("base2", dve.tensor_tensor(base2[:, :], base2[:, :], move[:, :], ALU.add))
                after("row")
                for k in range(TOPK):
                    chained(("pick", k), dve.scalar_tensor_tensor(
                        out=picked[:, k, :], in0=iota_e[:, :], scalar=expert_f[t][:, k:k + 1], in1=row[:, :],
                        op0=ALU.is_equal, op1=ALU.mult, accum_out=place[t][:, k:k + 1]))
                assert len(at) == PLACE_STEPS

            def places_to_int(n, t):
                dve.wait_ge(placed, PLACE_STEPS * (TPB * n + t + 1))
                dve.tensor_copy(place_i[t][:, :], place[t][:, :]).then_inc(place_ready, 1)

            pv = bank_o[:, 0:TPB * HP * VW].rearrange("p (h e) -> p h e", e=DH + 1)

            def sum_inverse(b):
                dve.wait_ge(pv_done, b + 1)
                dve.reciprocal(rsum[:, :], pv[:, :, DH]).then_inc(rsum_done, 1)

            def divide_by_sum(b):
                dve.wait_ge(rsum_done, b + 1)
                dve.tensor_tensor(o_s[:, :, :], pv[:, :, 0:DH], rsum[:, :].unsqueeze(2).to_broadcast([P, TPB * NH, DH]),
                                  ALU.mult).then_inc(o_ready, 1)

            def add_attention(b):
                dve.wait_ge(wo_done, b + 1)
                xt = xb[:, bass.ds(TPB * b, TPB), :]
                dve.tensor_tensor(xt, bank_o[:, TOK:2 * TOK].rearrange("p (t h) -> p t h", h=D), xt, ALU.add).then_inc(x2_done, 1)

            def residual_stats(n):
                for t in range(TPB):
                    stats(n, t, st2, st2_done)

            def first_stats(n, t):
                if t == 0:
                    dve.wait_ge(mv1_done, TPB * n)
                stats(n, t, st1, st1_done)

            def body(b, side):
                s0, s1, s2, so, s3, s4 = stages(b)
                if s3:
                    dve.wait_ge(x2_done, b - 1)
                if s2:
                    maxima(b, 0)
                if s3:
                    residual_stats(b - 2)
                    dve.wait_ge(st2_done, TPB * (b - 1))
                    dve.wait_ge(rstd_done, b + 2)
                if s0:
                    dve.wait_ge(st1_done, TPB * (b + 3))
                    dve.wait_ge(xc_ready, b + 2)
                if s2:
                    shift(b)
                    maxima(b, 1)
                if s3:
                    aggregate(st2, mv2, mv2_done)
                if s0:
                    aggregate(st1, mv1, mv1_done)
                if s2:
                    negate(b)
                if s4:
                    find_places(b - 3, 0)
                if so:
                    sum_inverse(b - 1)
                if s4:
                    places_to_int(b - 3, 0)
                if so:
                    divide_by_sum(b - 1)
                if s4:
                    find_places(b - 3, 1)
                nothing = lambda: None
                fillers = [(lambda: places_to_int(b - 3, 1)) if s4 else nothing, nothing,
                           (lambda: add_attention(b - 1)) if so else nothing, nothing]
                if not isinstance(b, int) or b + 3 < B:
                    fillers += [lambda: first_stats(b + 3, 0), nothing, lambda: first_stats(b + 3, 1)]
                if s3:
                    routing(b - 2, fillers)
                for step in fillers:
                    step()

            dve.wait_ge(x_first, 16)
            for t in range(TPB):
                stats(0, t, st1, st1_done)
            dve.wait_ge(st1_done, TPB)
            aggregate(st1, mv1, mv1_done)
            dve.tensor_copy(before_h[:, :], before[:, :])
            dve.wait_ge(const_in, 16 * NCONST)
            dve.tensor_scalar(bqs_s[:, :], bq_s[:, :], SCALE, None, ALU.mult).then_inc(dve_made, 1)
            dve.tensor_scalar(bv_rep[:, :], wo_s[:, :], 0.0, bv_s[:, 0:1], ALU.mult, ALU.add).then_inc(bvrep_ready, 1)
            dve.wait_ge(bias_done, 1)
            dve.tensor_tensor(bias_s[:, :], bank_o[:, 0:D], bo_s[:, :], ALU.add).then_inc(bias_ready, 1)
            dve.wait_ge(values_zeroed, 1)
            dve.memset(v_all[0:KV, :, :, DH:DH + 1], 1.0)
            dve.memset(v_all[KV:P, :, :, VW - 1:VW], 1.0)
            dve.wait_ge(x_rest, 16)
            dve.wait_ge(mv1_done, TPB)
            for t in range(TPB):
                stats(1, t, st1, st1_done)
            loop, last = phase1(body)
            with dve.Fori(loop.start, loop.stop, loop.step) as b:
                body(b, 0)
                body(b + 1, 1)
            for b in last:
                body(b, b % 2)

            def pack_experts(i, j, n):
                dve.wait_ge(page_in[j], 16 * (i + 1))
                if not (isinstance(n, int) and n == 0):
                    dve.wait_ge(packed, n)
                dve.tensor_tensor(digits[:, :], pg[j][0:1, :, EXPERT].bitcast(I32), digit[:, :], ALU.mult).then_inc(digits_done, 1)
                dve.wait_ge(digits_done, n + 1)
                with nc.allow_low_precision(reason="whole numbers below 2 ** 24 are exact in float32"):
                    dve.tensor_reduce(expert_i[j][:, :], digits[:, :], AX.X, ALU.add).then_inc(packed, 1)

            def quads(i, first, last):
                for j in range(SLOTS):
                    q = i * SLOTS + j
                    dve.wait_ge(act_ready, q + 1)
                    dve.tensor_tensor(h_s[j % 2][:, :, :], gu_ps[j % 2].rearrange("p (g u i) -> p g u i", g=QUAD, u=2)[:, :, 1, :],
                                      s_act[:, :, :], ALU.mult).then_inc(h_ready, 1)
                    if not first:
                        dve.wait_ge(y_out[j], 16 * QUAD * i)
                    dve.tensor_copy(scales[j][:, :], pg[j][:, :, WEIGHT])
                    dve.tensor_copy(codes[j][:, :], pg[j][:, :, CODE].bitcast(I32)).then_inc(code_ready, 1)
                    if j + 1 < SLOTS:
                        pack_experts(i, j + 1, q + 1)
                    elif not last:
                        pack_experts(i + 1, 0, q + 1)
                    if j == 2:
                        dve.wait_ge(sh_silu, i + 1)
                        dve.wait_ge(sh_up, i + 1)
                        dve.tensor_tensor(sh_h[:, :], bank_r[:, TOK:2 * TOK], sh_act[:, :], ALU.mult).then_inc(sh_ready, 1)
                    dve.wait_ge(ht_done, q + 1)
                    for a in range(2):
                        copied = dve.tensor_copy(h_t[j % 2][:, :, :].rearrange("p (g a) t -> p g a t", a=2)[:, :, a, :],
                                               bank_q[a * INTER:(a + 1) * INTER, 0:QUAD // 2 * P].rearrange(
                                                   "p (g t) -> p g t", t=P))
                    copied.then_inc(ht_ready, 1)
                dve.wait_ge(sh_done, i + 1)
                xt = xb[:, bass.ds(TPB * i, TPB), :]
                dve.tensor_tensor(xt, bank_w[:, 0:TOK].rearrange("p (t h) -> p t h", h=D), xt, ALU.add).then_inc(sh_added, 1)

            pack_experts(0, 0, 0)
            quads(0, True, False)
            with dve.Fori(1, NQ // SLOTS - 1) as i:
                quads(i, False, False)
            quads(NQ // SLOTS - 1, False, True)
            dve.wait_ge(sh_added, B)

            def combine(i, first):
                for j in range(SLOTS):
                    n = i * SLOTS + j
                    dve.wait_ge(ys_in[j], 16 * (i + 1))
                    if not (first and j == 0):
                        dve.wait_ge(summed, n)
                    dve.tensor_reduce(routed[:, :, :], ys[j].rearrange("p t k h -> p t h k"), AX.X, ALU.add).then_inc(added, 1)
                    dve.wait_ge(added, n + 1)
                    xt = xb[:, bass.ds(TPB * n, TPB), :]
                    dve.tensor_tensor(xt, routed[:, :, :], xt, ALU.add).then_inc(summed, 1)

            combine(0, True)
            with dve.Fori(1, B // SLOTS) as i:
                combine(i, False)


        @block.tensor
        def _(pe):
            def transposes(outs, ins, done):
                for o, i in zip(outs, ins):
                    k = i.shape[0]
                    last = pe.transpose(o, i, ident[0:k, 0:k])
                last.then_inc(done, 1)

            def mm(dst, w, v):
                return pe.matmul(dst, w, v, start=True, stop=True)

            def transpose_x(n):
                pe.wait_ge(xn_ready, TPB * (n + 1))
                pe.wait_ge(ctx_in, 32 * (n + 1))
                pe.wait_ge(q_ready, n)
                pe.wait_ge(vblk_ready, 2 * n)
                transposes([bank_q[:, t * P:(t + 1) * P] for t in range(TPB)] + [bank_q[0:DC, TOK:TOK + P]],
                           [xn[:, t, :] for t in range(TPB)] + [ctx_s[:, :]], xt_done)

            def project(n):
                pe.wait_ge(xts_ready, 2 * (n + 1))
                mm(bank_q[:, 0:TOK], wq_s[:, :], xn_t[:, :])
                mm(bank_q[:, TOK:TOK + KV], wk_s[:, :], ctx_t[:, 0:KV])
                mm(bank_q[:, TOK + KV:TOK + KV + D], ctx_t[:, :], wv_s[:, :]).then_inc(qkv_done, 1)

            def transpose_x2(n, side):
                pe.wait_ge(xn2_ready, TPB * (n + 1))
                pe.wait_ge(ranks_ready, n)
                transposes([bank_r[:, t * P:(t + 1) * P] for t in range(TPB)], [xn2[side][:, t, :] for t in range(TPB)], x2t_done)

            def logits(n):
                pe.wait_ge(x2t_ready, 2 * (n + 1))
                for t in range(TPB):
                    last = mm(bank_r[:, TOK + t * E:TOK + (t + 1) * E], x2_t[:, t * P:(t + 1) * P], gw_t[:, :])
                last.then_inc(logit_done, 1)

            def count_choosers(n):
                pe.wait_ge(chosen_ready, n + 1)
                m = chosen[:, :, :].rearrange("p t e -> p (t e)")
                mm(bank_r[:, 0:TPB * E], before_h[:, :], m)
                mm(bank_r[:, TPB * E:2 * TPB * E], ones_h[:, :], m).then_inc(ranks_done, 1)

            def gate_up_weights(w, slots):
                pe.wait_ge(raw_in, 48 * (w + 1))
                pe.wait_ge(wd_ready, 2 * w)
                transposes([bank_w[:, i * P:(i + 1) * P] for i in range(len(slots))], [raw_w[:, s, :] for s in slots], wgu_done)

            def down_weights(w):
                pe.wait_ge(wgu_ready, w + 2)
                transposes([bank_w[:, i * P:(i + 1) * P] for i in range(2)], [raw_w[:, 4 + i, :] for i in range(2)], wd_done)

            def scores(b, j):
                pe.wait_ge(q_ready, b + 1)
                pe.wait_ge(kexp_ready, b + 1)
                if not (isinstance(b, int) and b == 0):
                    pe.wait_ge(pt_ready, TPB * (b - 1) + j + 1)
                for half in range(2):
                    last = mm(bank_s[j][:, half * 512:(half + 1) * 512], q_t[:, j * P:(j + 1) * P],
                              k_exp[:, half * HP:(half + 1) * HP, :].rearrange("p h k -> p (h k)"))
                last.then_inc(scores_done, 1)

            def transpose_p(b, j):
                pe.wait_ge(p_ready, TPB * b + j + 1)
                transposes([bank_s[j][:, a * P:(a + 1) * P] for a in range(HP)],
                           [p_s[:, j, a * P:(a + 1) * P] for a in range(HP)], pt_done)

            def values(b, j):
                pe.wait_ge(pt_ready, TPB * b + j + 1)
                for a in range(HP):
                    at = (j * HP + a) * VW
                    last = mm(bank_o[:, at:at + VW], p_t[:, j, a * P:(a + 1) * P],
                              v_all[:, bass.ds(b, 1), a, :].rearrange("p b d -> p (b d)"))
                return last

            def body(b, side):
                s0, s1, s2, so, s3, s4 = stages(b)
                if s1:
                    transpose_x(b + 1)
                if s4:
                    count_choosers(b - 3)
                if so:
                    pe.wait_ge(vblk_ready, 2 * b)
                    pe.wait_ge(x2_done, b - 1)
                    values(b - 1, 0)
                if s1:
                    project(b + 1)
                if so:
                    values(b - 1, 1).then_inc(pv_done, 1)
                if s3:
                    transpose_x2(b - 2, side)
                if so:
                    pe.wait_ge(o_ready, b)
                    o_flat = o_s[:, :, :].rearrange("p h d -> p (h d)")
                    transposes([bank_o[:, t * P:(t + 1) * P] for t in range(TPB)],
                               [o_flat[:, t * P:(t + 1) * P] for t in range(TPB)], ot_done)
                if s2:
                    transpose_p(b, 0)
                if s3:
                    logits(b - 2)
                if so:
                    pe.wait_ge(ot_ready, b)
                    for t in range(TPB):
                        y = bank_o[:, TOK + t * D:TOK + (t + 1) * D]
                        pe.matmul(y, ident[:, :], bias_s[:, :], start=True, stop=False)
                        last = pe.matmul(y, o_t[:, t * P:(t + 1) * P], wo_s[:, :], start=False, stop=True)
                    last.then_inc(wo_done, 1)
                if s2:
                    transpose_p(b, 1)
                if s1:
                    scores(b + 1, 0)
                    scores(b + 1, 1)
                if s2:
                    gate_up_weights(b + 1, (0, 1, 2, 3))
                    down_weights(b + 1)

            pe.wait_ge(made, MADE)
            pe.wait_ge(gate_in, 16)
            transposes([bank_r[:, 0:E]], [gw_raw[:, :]], gwt_done)
            pe.wait_ge(bvrep_ready, 1)
            mm(bank_o[:, 0:D], bv_rep[:, :], wo_s[:, :]).then_inc(bias_done, 1)
            gate_up_weights(0, (0, 2))
            pe.wait_ge(wgu_ready, 2)
            transposes([bank_w[:, 0:P]], [raw_w[:, 4, :]], wd_done)
            pe.wait_ge(gwt_ready, 1)
            pe.wait_ge(bias_ready, 1)
            loop, last = phase1(body)
            with pe.Fori(loop.start, loop.stop, loop.step) as b:
                body(b, 0)
                body(b + 1, 1)
            for b in last:
                body(b, b % 2)

            def page_x(i, j):
                pe.wait_ge(page_in[j], 16 * (i + 1))
                transposes([xt_ps[j % 2][:, g * P:(g + 1) * P] for g in range(QUAD)], [pg[j][:, g, 0:D] for g in range(QUAD)],
                           pxt_done)

            def experts(j):
                v = nc.values_load(expert_i[j][0:1, 0:1], engines=(mybir.EngineType.PE,), min_val=0, max_val=E ** QUAD - 1,
                                   skip_runtime_bounds_check_because="it packs four results of max_index over E experts")
                return [(v // E ** g) % E for g in range(QUAD)]

            def gate_up(q, j, e):
                pe.wait_ge(pxt_ready, q + 1)
                for g in range(QUAD):
                    last = mm(gu_ps[j % 2][:, g * P:(g + 1) * P], pxt[j % 2][:, g * P:(g + 1) * P],
                              w_gu[:, bass.ds(e[g], 1), :].rearrange("p e i -> p (e i)"))
                last.then_inc(gu_done, 1)

            def transpose_h(q, j, first):
                pe.wait_ge(h_ready, q + 1)
                if not first:
                    pe.wait_ge(ht_ready, q)
                transposes([bank_q[:, g * P:(g + 1) * P] for g in range(QUAD // 2)],
                           [h_s[j % 2][:, 2 * g:2 * g + 2, :].rearrange("p g i -> p (g i)") for g in range(QUAD // 2)], ht_done)

            def down(q, j, e, first):
                pe.wait_ge(ht_ready, q + 1)
                if not first:
                    pe.wait_ge(y_ready, q)
                for g in range(QUAD):
                    last = mm(bank_o[:, g * D:(g + 1) * D], h_t[j % 2][:, g, :],
                              w_d[:, bass.ds(e[g], 1), :].rearrange("p e h -> p (e h)"))
                last.then_inc(y_done, 1)

            def quads(i, first, last):
                cols = bass.ds(i * TOK, TOK)
                q = i * SLOTS
                e = {0: experts(0)}
                for j in range(SLOTS):
                    gate_up(q + j, j, e[j])
                    if j == 0:
                        mm(bank_r[:, 0:TOK], sg_t[:, :], x_all[:, cols]).then_inc(sh_gate, 1)
                    if first and j == 1:
                        down(q, 0, e[0], True)
                    if j == 1:
                        pe.wait_ge(sh_silu, i + 1)
                        mm(bank_r[:, TOK:2 * TOK], su_t[:, :], x_all[:, cols]).then_inc(sh_up, 1)
                    if j + 1 < SLOTS:
                        page_x(i, j + 1)
                    elif not last:
                        page_x(i + 1, 0)
                    if j > 0 and not (first and j == 1):
                        down(q + j - 1, j - 1, e[j - 1], False)
                    if j + 1 < SLOTS or not last:
                        pe.wait_ge(packed, q + j + 2)
                    transpose_h(q + j, j, first and j == 0)
                    if j + 1 < SLOTS:
                        e[j + 1] = experts(j + 1)
                pe.wait_ge(sh_ready, i + 1)
                if not first:
                    pe.wait_ge(sh_added, i)
                for t in range(TPB):
                    end = mm(bank_w[:, t * D:(t + 1) * D], sh_h[:, t * P:(t + 1) * P], sd_t[:, :])
                end.then_inc(sh_done, 1)
                down(q + SLOTS - 1, SLOTS - 1, e[SLOTS - 1], False)

            pe.wait_ge(pt_ready, TPB * B)
            pe.wait_ge(x2_done, B)
            pe.wait_ge(ranks_ready, B)
            pe.wait_ge(wd_ready, 2 * (B + 1))
            pe.wait_ge(packed, 1)
            page_x(0, 0)
            quads(0, True, False)
            with pe.Fori(1, NQ // SLOTS - 1) as i:
                quads(i, False, False)
            quads(NQ // SLOTS - 1, False, True)


INPUTS = ["x", "ctx_768", "L0_xattn_Wq", "L0_xattn_bq", "L0_xattn_Wk", "L0_xattn_bk", "L0_xattn_Wv", "L0_xattn_bv",
          "L0_xattn_Wo", "L0_xattn_bo", "L0_ffn_gate_w", "L0_ffn_gate_bias", "L0_ffn_eg_w", "L0_ffn_eu_w",
          "L0_ffn_ed_w", "L0_ffn_sg_w", "L0_ffn_su_w", "L0_ffn_sd_w"]


def kernel(**inputs):
    import concourse.bacc as bacc
    from concourse.bass_utils import run_bass_kernel_spmd

    nc = bacc.Bacc("TRN2", target_bir_lowering=False, num_devices=1)
    arrays, args = {}, []
    for name in INPUTS:
        a = np.ascontiguousarray(inputs[name])
        arrays[f"in_{name}"] = a
        args.append(nc.dram_tensor(f"in_{name}", a.shape, mybir.dt.from_np(a.dtype), kind="ExternalInput").ap())
    args.append(nc.dram_tensor("out_x", (B, TOK, D), F32, kind="ExternalOutput").ap())
    args.append(nc.dram_tensor("pages", (PAGES * P, PC), F32, kind="Internal").ap())
    args.append(nc.dram_tensor("results", (B * TOK * TOPK, D), F32, kind="Internal").ap())
    build(nc, *args)
    return run_bass_kernel_spmd(nc, [arrays], core_ids=[0]).results[0]["out_x"]
```
